# Optimizing a Trainium2 kernel written in Bass

```python
import numpy as np
import jax
import jax.numpy as jnp

def _softmax(x, axis=-1):
    return jax.nn.softmax(x, axis=axis)

def _gelu(x):
    return jax.nn.gelu(x, approximate=True)

def _silu(x):
    return jax.nn.silu(x)

def _sigmoid(x):
    return jax.nn.sigmoid(x)

def _layernorm(x, axis=-1, eps=1e-05):
    m = jnp.mean(x, axis=axis, keepdims=True)
    v = jnp.var(x, axis=axis, keepdims=True)
    return (x - m) / jnp.sqrt(v + eps)

def _scatter_add(tgt, idx, src, axis=0):
    return tgt.at[idx].add(src)

def _segment_sum(src, seg, n):
    return jax.ops.segment_sum(src, seg, n)
kernel_name = 'mk_decoder_preln_d1_seqx_r4_562931'

def setup_inputs(seed: int=0):
    np.random.seed(seed)
    _w = jnp.asarray

    def _rec_inputs():
        import jax
        import jax.numpy as jnp
        _rk = jax.random.key(seed)
        x = -0.0003929 + 0.9999 * jax.random.normal(jax.random.fold_in(_rk, 1), (16, 256, 256), jnp.float32)
        _lenS = 256 - jax.random.randint(jax.random.fold_in(_rk, 7), (16,), 0, max(1, 256 // 4) + 1, jnp.int32)
        _lenS2 = 256 - jax.random.randint(jax.random.fold_in(_rk, 8), (16,), 0, max(1, 256 // 4) + 1, jnp.int32)
        _ctx_512P = jax.random.normal(jax.random.fold_in(_rk, 11), (16, 16, 128), jnp.float32)
        _ctx_512c = jax.random.dirichlet(jax.random.fold_in(_rk, 511), 0.3 * jnp.ones((16,), jnp.float32), (16, 256))
        _ctx_512t = jnp.einsum('bsk,bkd->bsd', _ctx_512c, _ctx_512P)
        _ctx_512t = _ctx_512t * jax.lax.rsqrt(jnp.mean(jnp.square(_ctx_512t)) + 1e-12) * 0.953939
        ctx_512 = 4.13588e-05 + 0.999923 * (_ctx_512t + 0.3 * jax.random.normal(jax.random.fold_in(_rk, 611), (16, 256, 128), jnp.float32))
        return (x, ctx_512)
    x, ctx_512 = _rec_inputs()

    def _L0_attn_setup():
        import jax, jax.numpy as jnp
        import numpy as np
        EPS = float(np.finfo(np.float32).eps)
        B, S, F_, E, H = (8, 1024, 256, 256, 16)
        HD = E // H
        LAYER = 1
        LAMBDA_INIT = 0.8 - 0.6 * float(np.exp(-0.3 * (LAYER - 1)))
        SCALE = 1.0 / float(np.sqrt(E // 2))

        def _rms(x, g):
            return x * jax.lax.rsqrt(jnp.mean(x * x, axis=-1, keepdims=True) + EPS) * g
        key = jax.random.key(seed)
        ks = jax.random.split(key, 7)
        x = jax.random.normal(ks[0], (B, S, F_), jnp.float32)
        s = 0.02
        Wq = jax.random.normal(ks[1], (E, F_), jnp.float32) * s
        Wk = jax.random.normal(ks[2], (E, F_), jnp.float32) * s
        Wv = jax.random.normal(ks[3], (E, F_), jnp.float32) * s
        W1 = jax.random.normal(ks[4], (E, E), jnp.float32) * s
        W2 = jax.random.normal(ks[5], (E, E), jnp.float32) * s
        lambda_params = jnp.full((4,), 0.8, jnp.float32)
        g1 = jnp.ones((F_,), jnp.float32)
        g2 = jnp.ones((HD,), jnp.float32)
        g3 = jnp.ones((E,), jnp.float32)
        return dict(x=x, Wq=Wq, Wk=Wk, Wv=Wv, lambda_params=lambda_params, g1=g1, g2=g2, g3=g3, W1=W1, W2=W2)
    _L0_attn_all = _L0_attn_setup()
    _L0_attn_in = {k: v for k, v in _L0_attn_all.items() if k in ('Wq', 'Wk', 'Wv', 'lambda_params', 'g1', 'g2', 'g3', 'W1', 'W2')}
    del _L0_attn_all

    def _L0_xattn_setup():
        import jax, jax.numpy as jnp
        import numpy as np
        B, LQ, LK = (8, 512, 512)
        QD, KD, VD = (256, 128, 128)
        key = jax.random.key(seed)
        ks = jax.random.split(key, 9)
        s = 0.02
        return {'query': jax.random.normal(ks[0], (B, LQ, QD), jnp.float32), 'key': jax.random.normal(ks[1], (B, LK, KD), jnp.float32), 'value': jax.random.normal(ks[2], (B, LK, VD), jnp.float32), 'Wq': jax.random.normal(ks[3], (QD, QD), jnp.float32) * s, 'bq': jnp.zeros((QD,), jnp.float32), 'Wk': jax.random.normal(ks[4], (KD, QD), jnp.float32) * s, 'bk': jnp.zeros((QD,), jnp.float32), 'Wv': jax.random.normal(ks[5], (VD, QD), jnp.float32) * s, 'bv': jnp.zeros((QD,), jnp.float32)}
    _L0_xattn_all = _L0_xattn_setup()
    _L0_xattn_in = {k: v for k, v in _L0_xattn_all.items() if k in ('Wq', 'bq', 'Wk', 'bk', 'Wv', 'bv')}
    del _L0_xattn_all

    def _L0_ffn_setup():
        import jax, jax.numpy as jnp
        import numpy as np
        B, S, D_MODEL, D_FF, E, R, TOP_K = (4, 512, 256, 1024, 8, 16, 2)
        key = jax.random.key(seed)
        ks = jax.random.split(key, 9)
        sd = 1.0 / np.sqrt(D_MODEL)
        return {'hidden_states': jax.random.normal(ks[0], (B, S, D_MODEL), jnp.float32), 'wi': jax.random.normal(ks[1], (D_FF, D_MODEL), jnp.float32) * sd, 'bi': jax.random.normal(ks[2], (D_FF,), jnp.float32) * 0.01, 'wo': jax.random.normal(ks[3], (D_MODEL, D_FF), jnp.float32) * (1.0 / np.sqrt(D_FF)), 'bo': jax.random.normal(ks[4], (D_MODEL,), jnp.float32) * 0.01, 'lora_A': jax.random.normal(ks[5], (E, R, D_MODEL), jnp.float32) * sd, 'lora_B': jax.random.normal(ks[6], (E, D_FF, R), jnp.float32) * 0.02, 'gate_w': jax.random.normal(ks[7], (E, D_MODEL), jnp.float32) * sd, 'gate_b': jax.random.normal(ks[8], (E,), jnp.float32) * 0.01}
    _L0_ffn_all = _L0_ffn_setup()
    _L0_ffn_in = {k: v for k, v in _L0_ffn_all.items() if k in ('wi', 'bi', 'wo', 'bo', 'lora_A', 'lora_B', 'gate_w', 'gate_b')}
    del _L0_ffn_all
    return {'x': x, 'ctx_512': ctx_512, 'L0_attn_Wq': _L0_attn_in['Wq'], 'L0_attn_Wk': _L0_attn_in['Wk'], 'L0_attn_Wv': _L0_attn_in['Wv'], 'L0_attn_lambda_params': _L0_attn_in['lambda_params'], 'L0_attn_g1': _L0_attn_in['g1'], 'L0_attn_g2': _L0_attn_in['g2'], 'L0_attn_g3': _L0_attn_in['g3'], 'L0_attn_W1': _L0_attn_in['W1'], 'L0_attn_W2': _L0_attn_in['W2'], 'L0_xattn_Wq': _L0_xattn_in['Wq'], 'L0_xattn_bq': _L0_xattn_in['bq'], 'L0_xattn_Wk': _L0_xattn_in['Wk'], 'L0_xattn_bk': _L0_xattn_in['bk'], 'L0_xattn_Wv': _L0_xattn_in['Wv'], 'L0_xattn_bv': _L0_xattn_in['bv'], 'L0_ffn_wi': _L0_ffn_in['wi'], 'L0_ffn_bi': _L0_ffn_in['bi'], 'L0_ffn_wo': _L0_ffn_in['wo'], 'L0_ffn_bo': _L0_ffn_in['bo'], 'L0_ffn_lora_A': _L0_ffn_in['lora_A'], 'L0_ffn_lora_B': _L0_ffn_in['lora_B'], 'L0_ffn_gate_w': _L0_ffn_in['gate_w'], 'L0_ffn_gate_b': _L0_ffn_in['gate_b']}

def reference(x, ctx_512, L0_attn_Wq, L0_attn_Wk, L0_attn_Wv, L0_attn_lambda_params, L0_attn_g1, L0_attn_g2, L0_attn_g3, L0_attn_W1, L0_attn_W2, L0_xattn_Wq, L0_xattn_bq, L0_xattn_Wk, L0_xattn_bk, L0_xattn_Wv, L0_xattn_bv, L0_ffn_wi, L0_ffn_bi, L0_ffn_wo, L0_ffn_bo, L0_ffn_lora_A, L0_ffn_lora_B, L0_ffn_gate_w, L0_ffn_gate_b):
    import jax
    import jax.numpy as jnp

    def _L0_attn_ref(x, Wq, Wk, Wv, lambda_params, g1, g2, g3, W1, W2):
        import jax, jax.numpy as jnp
        import numpy as np
        EPS = float(np.finfo(np.float32).eps)
        B, S, F_, E, H = (8, 1024, 256, 256, 16)
        HD = E // H
        LAYER = 1
        LAMBDA_INIT = 0.8 - 0.6 * float(np.exp(-0.3 * (LAYER - 1)))
        SCALE = 1.0 / float(np.sqrt(E // 2))

        def _rms(x, g):
            return x * jax.lax.rsqrt(jnp.mean(x * x, axis=-1, keepdims=True) + EPS) * g
        b, s_len, _ = x.shape
        xn = _rms(x, g1)
        Q = jnp.einsum('bsf,ef->bse', xn, Wq).reshape(b, s_len, H, HD)
        K = jnp.einsum('bsf,ef->bse', xn, Wk).reshape(b, s_len, H, HD)
        V = jnp.einsum('bsf,ef->bse', xn, Wv).reshape(b, s_len, H, HD)
        pQ = jax.nn.elu(Q)
        pK = jax.nn.elu(K)
        Q1, Q2 = jnp.split(pQ, 2, axis=-1)
        K1, K2 = jnp.split(pK, 2, axis=-1)
        kv1 = jnp.einsum('bshe,bshd->bsed', K1, V) * SCALE
        kv2 = jnp.einsum('bshe,bshd->bsed', K2, V) * SCALE
        w1 = jnp.einsum('bshe,bsed->bshd', Q1, kv1)
        w2 = jnp.einsum('bshe,bsed->bshd', Q2, kv2)
        lmb = jnp.exp(lambda_params[0] * lambda_params[1]) - jnp.exp(lambda_params[2] * lambda_params[3]) + LAMBDA_INIT
        attn = w1 - lmb * w2
        attn = (1.0 - LAMBDA_INIT) * _rms(attn, g2)
        attn = attn.reshape(b, s_len, E)
        attn = _rms(attn, g3) + attn
        h = jax.nn.gelu(jnp.einsum('bse,fe->bsf', attn, W1), approximate=False)
        out = jnp.einsum('bsf,ef->bse', h, W2) + attn
        return out

    def _L0_xattn_ref(query, key, value, Wq, bq, Wk, bk, Wv, bv):
        import jax, jax.numpy as jnp
        import numpy as np
        B, LQ, LK = (8, 512, 512)
        QD, KD, VD = (256, 128, 128)
        q = jnp.einsum('bld,de->ble', query, Wq) + bq
        k = jnp.einsum('bld,de->ble', key, Wk) + bk
        v = jnp.einsum('bld,de->ble', value, Wv) + bv
        scores = jnp.einsum('bqe,bke->bqk', q, k)
        attn = jax.nn.softmax(scores, axis=-1)
        out = jnp.einsum('bqk,bke->bqe', attn, v)
        return out

    def _L0_ffn_ref(hidden_states, wi, bi, wo, bo, lora_A, lora_B, gate_w, gate_b):
        import jax, jax.numpy as jnp
        import numpy as np
        B, S, D_MODEL, D_FF, E, R, TOP_K = (4, 512, 256, 1024, 8, 16, 2)
        logits = jnp.einsum('bsd,ed->bse', hidden_states, gate_w) + gate_b
        scores = jax.nn.softmax(logits, axis=-1)
        top_v, top_i = jax.lax.top_k(scores, TOP_K)
        val_sum = top_v.sum(axis=-1)
        out = jnp.zeros_like(hidden_states)
        for e in range(E):
            count = (top_i == e).sum(axis=-1).astype(hidden_states.dtype)
            gate = count * val_sum
            inter = jnp.einsum('bsd,fd->bsf', hidden_states, wi) + bi + jnp.einsum('bsr,fr->bsf', jnp.einsum('bsd,rd->bsr', hidden_states, lora_A[e]), lora_B[e])
            h = jax.nn.relu(inter)
            expert_out = jnp.einsum('bsf,df->bsd', h, wo) + bo
            out = out + gate[..., None] * expert_out
        return out
    x = x + _L0_attn_ref(_layernorm(x, axis=-1), L0_attn_Wq, L0_attn_Wk, L0_attn_Wv, L0_attn_lambda_params, L0_attn_g1, L0_attn_g2, L0_attn_g3, L0_attn_W1, L0_attn_W2)
    x = x + _L0_xattn_ref(_layernorm(x, axis=-1), ctx_512, ctx_512, L0_xattn_Wq, L0_xattn_bq, L0_xattn_Wk, L0_xattn_bk, L0_xattn_Wv, L0_xattn_bv)
    x = x + _L0_ffn_ref(_layernorm(x, axis=-1), L0_ffn_wi, L0_ffn_bi, L0_ffn_wo, L0_ffn_bo, L0_ffn_lora_A, L0_ffn_lora_B, L0_ffn_gate_w, L0_ffn_gate_b)
    return x

_drawn_inputs = setup_inputs


def setup_inputs(seed=0):
    import zlib

    import numpy as np

    out = dict(_drawn_inputs(seed))
    spreads = {'L0_attn_lambda_params': (0.800000011920929, 0.2),
     'L0_attn_g1': (1.0, 0.2),
     'L0_attn_g2': (1.0, 0.2),
     'L0_attn_g3': (1.0, 0.2),
     'L0_xattn_bq': (0.0, 0.8),
     'L0_xattn_bk': (0.0, 0.8),
     'L0_xattn_bv': (0.0, 0.1)}
    factors = {'L0_ffn_bi': 8.0,
     'L0_ffn_bo': 8.0,
     'L0_ffn_lora_A': 2.816,
     'L0_ffn_lora_B': 2.797,
     'L0_ffn_gate_b': 8.0}
    for name, (base, spread) in spreads.items():
        noise = np.random.default_rng([zlib.crc32(name.encode()), seed]).standard_normal(out[name].shape)
        drawn = base * np.exp(spread * noise) if base else spread * noise
        out[name] = jnp.asarray(drawn.astype(out[name].dtype))
    for name, factor in factors.items():
        out[name] = (out[name] * factor).astype(out[name].dtype)
    return out
```

```python
from contextlib import ExitStack

import numpy as np

import concourse.bass as bass
from concourse import mybir

F32 = mybir.dt.float32
F32R = mybir.dt.float32r
BF16 = mybir.dt.bfloat16
ALU = mybir.AluOpType
ACT = mybir.ActivationFunctionType
AX_X = mybir.AxisListType.X

P = 128
UNITS = 16
T = 256
TT = T // P
D = 256
KD = D // P
H, HD = 16, 16
GT = P // H
GROUPS = T // GT
C = 128
FF = 1024
FT = FF // P
EX, R = 8, 16
LN_EPS = 1e-5
RMS_EPS = float(np.finfo(np.float32).eps)
LAMBDA_INIT = 0.8 - 0.6 * float(np.exp(-0.3 * (1 - 1)))
HEAD_SCALE = 1.0 / float(np.sqrt(D // 2))


SLOT_FULL = 16 * (UNITS // 2)


class Unit:

    def __init__(self, pair, offset, least):
        self.pair, self.offset = pair, offset
        self.index = 2 * pair + offset
        self.slot = offset % 2
        self.turn = pair + offset // 2
        self.least = least

    def has(self, back):
        return self.least >= back

    def before(self, back):
        return Unit(self.pair, self.offset - back, self.least - back)


def nth(u, per_unit, k, loops=0):
    return u.index * per_unit + (k + loops * UNITS * per_unit)


def landed(u, dmas=1, loops=0):
    return u.turn * (16 * dmas) + 16 * dmas + loops * SLOT_FULL * dmas


def over_units(eng, units, stages):
    last = max(lag for lag, _ in stages)
    deepest = 4 if last <= 2 else 6
    assert last + 2 <= deepest and units % 2 == 0

    def step(t, pair=None):
        for lag, emit in stages:
            if pair is not None:
                emit(Unit(pair, t - lag, deepest - lag))
            elif 0 <= t - lag < units:
                emit(Unit(0, t - lag, t - lag))

    for t in range(deepest):
        step(t)
    with eng.Fori(deepest // 2, units // 2) as pair:
        for t in range(2):
            step(t, pair)
    for t in range(units, units + last):
        step(t)


def decoder(nc, x, ctx_512, Wq, Wk, Wv, lam, g1, g2, g3, W1, W2,
            xWq, xbq, xWk, xbk, xWv, xbv, wi, bi, wo, bo, lora_A, lora_B, gate_w, gate_b, out):
    assert x.shape == (UNITS, T, D)
    with ExitStack() as ctx:
        names = set()

        def sb(name, shape, dt=F32, where=ctx):
            return where.enter_context(nc.sbuf_tensor(name, shape, dt))

        def sem(name):
            assert name not in names
            names.add(name)
            return ctx.enter_context(nc.semaphore(name))

        bank = [ctx.enter_context(nc.psum_tensor(f"bank{i}", [P, 512], F32)) for i in range(8)]

        def pair(name, shape, where=ctx):
            return [sb(name + "_hi", shape, F32R, where), sb(name + "_lo", shape, F32R, where)]

        wqkvT = pair("wqkvT", [P, KD, 3 * D])
        w1T = pair("w1T", [P, KD, D])
        w2T = pair("w2T", [P, KD, D])
        mT = pair("mT", [P, KD, C])
        xwv = pair("xwv", [P, D])
        wiT = pair("wiT", [P, KD, FF])
        woT = pair("woT", [P, FT, D])
        laT = pair("laT", [P, KD, P])
        lbT = pair("lbT", [P, FF])
        gwT = pair("gwT", [P, KD, P])
        identf = sb("identf", [P, P])
        identb = sb("identb", [P, P], BF16)
        g1c = sb("g1c", [P, KD])
        g2row = sb("g2row", [P, H, HD])
        g3row = sb("g3row", [P, D])
        bvrow = sb("bvrow", [P, D])
        gbrow = sb("gbrow", [P, EX])
        bic = sb("bic", [P, FT])
        wbkrow = sb("wbkrow", [P, D])
        bqbk = sb("bqbk", [P, 1])
        bqk = sb("bqk", [P, 1])
        qfac = sb("qfac", [P, 1])
        slotmask = sb("slotmask", [P, GT])
        tril = sb("tril", [P, EX, EX])
        mhalf = sb("mhalf", [P, GROUPS])

        qkv_d = nc.dram_tensor("qkv_scratch", (3, UNITS, T, D), F32).ap()
        w_d = nc.dram_tensor("attn_scratch", (UNITS, T, D), F32).ap()
        x1_d = nc.dram_tensor("x1_scratch", (UNITS, T, D), F32).ap()
        x2_d = nc.dram_tensor("x2_scratch", (UNITS, T, D), F32).ap()

        def tiles(dram):
            return dram.rearrange("u (i p) f -> u p i f", p=P)

        x_t, x1_t, x2_t, out_t, ctx_t = map(tiles, (x, x1_d, x2_d, out, ctx_512))

        with ExitStack() as a:
            n_in = sb("n_in", [P, 2, D], F32, a)
            nat = {"q": n_in}
            for key in ("k", "v", "w1", "w2", "xq"):
                nat[key] = sb("n_" + key, [P, 2, D], F32, a)
            nat["xk"] = sb("n_xk", [P, 1, D], F32, a)
            nat["xv"] = sb("n_xv", [P, 1, D], F32, a)
            nat["wi"] = sb("n_wi", [P, FT, D], F32, a)
            nat["wo"] = sb("n_wo", [P, 2, FF], F32, a)
            nat["la"] = sb("n_la", [P, 1, D], F32, a)
            nat["gw"] = sb("n_gw", [P, 1, D], F32, a)
            nat["lb"] = sb("n_lb", [P, FT, EX, R], F32, a)
            stage = sb("stage", [P, 2, 512], F32, a)
            lamt = sb("lamt", [P, 4], F32, a)
            lprod = sb("lprod", [P, 2], F32, a)
            lexp = sb("lexp", [P, 2], F32, a)
            ldiff = sb("ldiff", [P, 1], F32, a)
            g2raw = sb("g2raw", [P, H, HD], F32, a)
            bqc = sb("bqc", [P, 2], F32, a)
            bkc = sb("bkc", [P, 2], F32, a)
            bkwide = sb("bkwide", [P, 2, P], F32, a)
            onesw = sb("onesw", [P, P], F32, a)
            xqT = sb("xqT", [P, 2, D], F32, a)
            xkT = sb("xkT", [P, 2, C], F32, a)
        s_w = {k: sem("w_" + k) for k in ("early", "late", "small")}
        s_const, s_cleared = sem("const_made"), sem("const_cleared")
        s_gclear = sem("gate_cleared")
        s_turn = sem("weight_turned")
        s_stage = sem("weight_staged")
        s_whi = sem("weight_hi")
        s_wlo = sem("weight_lo")
        s_lam = sem("lambda_step")
        s_lamexp = sem("lambda_exp")
        s_small = sem("small_made")
        s_fold = sem("fold_turned")
        s_foldc = sem("fold_copied")
        s_foldm = sem("fold_product")
        s_folde = sem("fold_evacuated")
        s_foldlo = sem("fold_lo")

        ln_in = [sem(f"ln_in{i}") for i in range(2)]
        ln_stats, ln_var, ln_ved, ln_rstd = sem("ln_stats"), sem("ln_var"), sem("ln_var_eps"), sem("ln_rstd")
        ln_norm, ln_turned, ln_hi, ln_lo = sem("ln_norm"), sem("ln_turned"), sem("ln_hi"), sem("ln_lo")
        a_stored = [sem(f"a_stored{i}") for i in range(2)]
        stored = [sem(f"stored{i}") for i in range(2)]

        with ExitStack() as a:
            xin = sb("xin", [P, 2, TT, D], F32, a)
            a_st = sb("a_st", [P, 2, TT, 6], F32, a)
            a_mv = sb("a_mv", [P, 2, TT, 2], F32, a)
            a_ve = sb("a_ve", [P, 2, TT], F32, a)
            a_rs = sb("a_rs", [P, 2, TT], F32, a)
            a_xn = sb("a_xn", [P, 2, TT, D], F32, a)
            a_xT = [pair(f"a_xT{i}", [P, KD, T], a) for i in range(2)]
            a_exp = sb("a_exp", [P, 2, 512], F32, a)
            a_elu = sb("a_elu", [P, 2, 512], F32, a)
            a_out = sb("a_out", [P, 2, TT, 3 * D], F32, a)
        a_qk, a_v, a_negd, a_expd = sem("a_qk"), sem("a_v"), sem("a_negd"), sem("a_expd")
        a_elud, a_fin, a_vcopy = sem("a_elud"), sem("a_fin"), sem("a_vcopy")

        with ExitStack() as a:
            h_k = sb("h_k", [P, 2, 512], F32, a)
            h_v = sb("h_v", [P, 2, 512], F32, a)
            h_q = sb("h_q", [P, 2, 512], F32, a)
            h_kp = sb("h_kp", [P, 3, 512], BF16, a)
            h_qp = sb("h_qp", [P, 3, 512], BF16, a)
            h_vp = sb("h_vp", [P, 2, 3, 512], BF16, a)
            h_mp = sb("h_mp", [P, 2, 3, 512], BF16, a)
            h_r = sb("h_r", [P, 3, 512], F32, a)
            h_w = sb("h_w", [P, 512], F32, a)
            h_qd = sb("h_qd", [P, 2, 3, GT, 512], BF16, a)
            h_kd = sb("h_kd", [P, 2, 3, GT, 512], BF16, a)
        h_kin = [sem(f"h_kin{i}") for i in range(2)]
        h_vin = [sem(f"h_vin{i}") for i in range(2)]
        h_qin = [sem(f"h_qin{i}") for i in range(2)]
        h_part = {k: [sem(f"h_{k}_{s}") for s in ("p1", "rest", "p2", "p3")] for k in "kvqm"}
        h_zeroed = sem("h_zeroed")
        h_kdd = [sem(f"h_kdd{i}") for i in range(2)]
        h_qdd = sem("h_qdd")
        h_kv, h_out, h_wd = sem("h_kv"), sem("h_out"), sem("h_wd")

        with ExitStack() as a:
            m_w = sb("m_w", [P, 2, TT, D], F32, a)
            m_x = sb("m_x", [P, 2, TT, D], F32, a)
            m_sq = sb("m_sq", [P, TT, D], F32, a)
            m_ss = sb("m_ss", [P, TT * H], F32, a)
            m_ms = sb("m_ms", [P, 2, TT * H], F32, a)
            m_rh = sb("m_rh", [P, 2, TT * H], F32, a)
            m_n1 = sb("m_n1", [P, TT, D], F32, a)
            m_at = sb("m_at", [P, TT, D], F32, a)
            m_s3 = sb("m_s3", [P, TT], F32, a)
            m_m3 = sb("m_m3", [P, TT], F32, a)
            m_r3 = sb("m_r3", [P, TT], F32, a)
            m_t3 = sb("m_t3", [P, TT, D], F32, a)
            m_a2 = sb("m_a2", [P, 2, TT, D], F32, a)
            m_xa = sb("m_xa", [P, 2, TT, D], F32, a)
            m_aT = [pair(f"m_aT{i}", [P, KD, T], a) for i in range(2)]
            m_g = sb("m_g", [P, 2, 512], F32, a)
            m_hT = [pair(f"m_hT{i}", [P, KD, T], a) for i in range(2)]
            m_y = sb("m_y", [P, 2, TT, D], F32, a)
        m_win = [sem(f"m_win{i}") for i in range(2)]
        m_xin = [sem(f"m_xin{i}") for i in range(2)]
        m_sqd, m_ssd, m_msd, m_rhd = sem("m_sqd"), sem("m_ssd"), sem("m_msd"), sem("m_rhd")
        m_n1d, m_atd, m_s3d, m_m3d, m_r3d = sem("m_n1d"), sem("m_atd"), sem("m_s3d"), sem("m_m3d"), sem("m_r3d")
        m_t3d, m_a2d, m_xad = sem("m_t3d"), sem("m_a2d"), sem("m_xad")
        m_turned, m_hi, m_lo = sem("m_turned"), sem("m_hi"), sem("m_lo")
        m_h, m_gelu, m_ghi, m_glo = sem("m_h"), sem("m_gelu"), sem("m_ghi"), sem("m_glo")
        m_o, m_yd = sem("m_o"), sem("m_yd")

        with ExitStack() as a:
            c_x = sb("c_x", [P, 2, TT, D], F32, a)
            c_c = sb("c_c", [P, 2, TT, C], F32, a)
            c_st = sb("c_st", [P, 2, TT, 6], F32, a)
            c_mv = sb("c_mv", [P, 2, TT, 2], F32, a)
            c_ve = sb("c_ve", [P, 2, TT], F32, a)
            c_rs = sb("c_rs", [P, 2, TT], F32, a)
            c_xn = sb("c_xn", [P, 2, TT, D], F32, a)
            c_xb = sb("c_xb", [P, 2, TT, D], F32, a)
            c_rr = sb("c_rr", [P, TT, D], F32, a)
            c_r = sb("c_r", [P, 2, TT], F32, a)
            c_xT = [pair(f"c_xT{i}", [P, KD, T], a) for i in range(2)]
            c_ch = [pair(f"c_ch{i}", [P, TT, C], a) for i in range(2)]
            c_cT = [pair(f"c_cT{i}", [P, T], a) for i in range(2)]
            c_uT = [pair(f"c_uT{i}", [P, T], a) for i in range(2)]
            c_mx = sb("c_mx", [P, TT], F32, a)
            c_mr = sb("c_mr", [P, TT], F32, a)
            c_nb = sb("c_nb", [P, TT], F32, a)
            c_p = sb("c_p", [P, TT, T], F32, a)
            c_sum = sb("c_sum", [P, TT], F32, a)
            c_inv = sb("c_inv", [P, TT], F32, a)
            c_pT = pair("c_pT", [P, TT, T], a)
            c_oT = pair("c_oT", [P, T], a)
            c_y = sb("c_y", [P, 2, TT, D], F32, a)
        c_cin = [sem(f"c_cin{i}") for i in range(2)]
        c_xbd, c_rrd, c_rd = sem("c_xbd"), sem("c_rrd"), sem("c_rd")
        c_cturned, c_chi, c_clo = sem("c_cturned"), sem("c_chi"), sem("c_clo")
        c_cnhi, c_cnlo = sem("c_cnhi"), sem("c_cnlo")
        c_u, c_uhi, c_ulo = sem("c_u"), sem("c_uhi"), sem("c_ulo")
        c_s, c_mxd, c_mrd, c_nbd, c_pd, c_invd = sem("c_s"), sem("c_mxd"), sem("c_mrd"), sem("c_nbd"), sem("c_pd"), sem("c_invd")
        c_pturned, c_phi, c_plo = sem("c_pturned"), sem("c_phi"), sem("c_plo")
        c_o, c_ohi, c_olo = sem("c_o"), sem("c_ohi"), sem("c_olo")
        c_f, c_yd = sem("c_f"), sem("c_yd")

        with ExitStack() as a:
            borow = sb("borow", [P, D], F32, a)
            f_x = sb("f_x", [P, 2, TT, D], F32, a)
            f_st = sb("f_st", [P, 2, TT, 6], F32, a)
            f_mv = sb("f_mv", [P, 2, TT, 2], F32, a)
            f_ve = sb("f_ve", [P, 2, TT], F32, a)
            f_rs = sb("f_rs", [P, 2, TT], F32, a)
            f_xn = sb("f_xn", [P, 2, TT, D], F32, a)
            f_xT = [pair(f"f_xT{i}", [P, KD, T], a) for i in range(2)]
            f_lT = sb("f_lT", [P, T], F32, a)
            f_a = sb("f_a", [P, 2, T], F32, a)
            f_lg = sb("f_lg", [P, TT, EX], F32, a)
            f_mx = sb("f_mx", [P, TT], F32, a)
            f_sh = sb("f_sh", [P, TT, EX], F32, a)
            f_ex = sb("f_ex", [P, TT, EX], F32, a)
            f_sm = sb("f_sm", [P, TT], F32, a)
            f_iv = sb("f_iv", [P, TT], F32, a)
            f_sc = sb("f_sc", [P, TT, EX], F32, a)
            f_gt = sb("f_gt", [P, TT, EX, EX], F32, a)
            f_eq = sb("f_eq", [P, TT, EX, EX], F32, a)
            f_rk = sb("f_rk", [P, TT, EX], F32, a)
            f_top = sb("f_top", [P, TT, EX], F32, a)
            f_vs = sb("f_vs", [P, 2, TT], F32, a)
            f_vk = sb("f_vk", [P, 2, TT], F32, a)
            f_vs2 = sb("f_vs2", [P, TT], F32, a)
            f_bo = sb("f_bo", [P, TT, D], F32, a)
            f_xb = sb("f_xb", [P, 2, TT, D], F32, a)
            f_m = sb("f_m", [P, 2, TT, EX, R], BF16, a)
            f_ad = sb("f_ad", [P, 2, T], F32, a)
            f_adT = [pair(f"f_adT{i}", [P, 2, T], a) for i in range(2)]
            f_h1 = sb("f_h1", [P, 2, 512], F32, a)
            f_h2 = sb("f_h2", [P, 2, 512], F32, a)
            f_hs = sb("f_hs", [P, 2, 512], F32, a)
            f_hT = [pair(f"f_hT{i}", [P, FT, T], a) for i in range(2)]
            f_y = sb("f_y", [P, 2, TT, D], F32, a)
        f_la, f_lTd, f_ad_, f_lturned = sem("f_la"), sem("f_lTd"), sem("f_acopied"), sem("f_lturned")
        f_top1, f_exd, f_top2, f_vsd, f_md = sem("f_top1"), sem("f_exd"), sem("f_top2"), sem("f_vsd"), sem("f_md")
        f_mT, f_adm, f_adhi, f_adlo = sem("f_mT"), sem("f_adm"), sem("f_adhi"), sem("f_adlo")
        f_bod, f_xbd = sem("f_bod"), sem("f_xbd")
        f_base, f_more = sem("f_base"), sem("f_more")
        f_h1d, f_h2d, f_hsd, f_hhi, f_hlo = sem("f_h1d"), sem("f_h2d"), sem("f_hsd"), sem("f_hhi"), sem("f_hlo")
        f_vkd, f_o, f_yd = sem("f_vkd"), sem("f_o"), sem("f_yd")

        def blocks(key, rows, k):
            return [nat[key][:, m, k * P:(k + 1) * P] for m in rows]

        jobs = []
        for k in range(KD):
            jobs.append((blocks("q", (0, 1), k) + blocks("k", (0, 1), k), wqkvT, (k, 0, 512), k))
        for k in range(KD):
            jobs.append((blocks("v", (0, 1), k), wqkvT, (k, 512, 768), k))
        for key, dst in (("w1", w1T), ("w2", w2T)):
            jobs.append((blocks(key, (0, 1), 0) + blocks(key, (0, 1), 1), dst, None, None))
        EARLY = len(jobs)
        for k in range(KD):
            for half in range(2):
                jobs.append((blocks("wi", range(4 * half, 4 * half + 4), k), wiT, (k, 512 * half, 512 * half + 512), None))
        for j in range(0, FT, 2):
            jobs.append((blocks("wo", (0, 1), j) + blocks("wo", (0, 1), j + 1), woT, ("rows", j), None))
        jobs.append((blocks("la", (0,), 0) + blocks("la", (0,), 1), laT, None, None))
        jobs.append((blocks("gw", (0,), 0) + blocks("gw", (0,), 1), gwT, None, None))
        for half in range(2):
            jobs.append(([nat["lb"][:, j].rearrange("p e r -> p (e r)") for j in range(4 * half, 4 * half + 4)],
                         lbT, ("flat", 512 * half), None))

        def target(part, at):
            if at is None:
                return part[:, :, :].rearrange("p a b -> p (a b)")
            if at[0] == "rows":
                return part[:, at[1]:at[1] + 2, :].rearrange("p a b -> p (a b)")
            if at[0] == "flat":
                return part[:, at[1]:at[1] + 512]
            return part[:, at[0], at[1]:at[2]]

        N_EARLY, N_SMALL, N_LATE = 9, 9, 12

        f_chain = sem("f_chain")
        s_passed = sem("waits_passed")

        def apart(eng):
            eng.sem_inc(s_passed, 1)

        def flat(ap):
            return ap.rearrange("p a b -> p (a b)")

        def by_e(ap):
            return ap.rearrange("p (g e) -> p e g", e=HD)

        def in_e(ap):
            return ap.rearrange("p (e g) -> p e g", e=HD)

        block = ctx.enter_context(nc.Block())

        @block.sync
        def _(sp):
            loads = [(nat["q"][:, m, :], Wq.rearrange("(h e) f -> e h f", e=HD)[8 * m:8 * m + 8]) for m in range(2)]
            loads += [(nat[k], w.rearrange("(m p) f -> p m f", p=P)) for k, w in
                      (("k", Wk), ("v", Wv), ("w1", W1), ("w2", W2), ("xq", xWq), ("xk", xWk), ("xv", xWv))]
            for dst, src in loads:
                sp.dma_start(dst if len(dst.shape) < 3 else dst[:, :, :], src).then_inc(s_w["early"], 16)
            small = [(g1c[:, :], g1.rearrange("(k p) -> p k", p=P)),
                     (lamt[:, :], lam.rearrange("(a n) -> a n", a=1).broadcast_to([P, 4])),
                     (g3row[:, :], g3.rearrange("(a n) -> a n", a=1).broadcast_to([P, D])),
                     (bvrow[:, :], xbv.rearrange("(a n) -> a n", a=1).broadcast_to([P, D])),
                     (gbrow[:, :], gate_b.rearrange("(a n) -> a n", a=1).broadcast_to([P, EX])),
                     (g2raw[:, 0, :], g2.rearrange("(a n) -> a n", a=1).broadcast_to([P, HD])),
                     (bic[:, :], bi.rearrange("(k p) -> p k", p=P)),
                     (bqc[:, :], xbq.rearrange("(k p) -> p k", p=P)),
                     (bkc[:, :], xbk.rearrange("(k p) -> p k", p=P))]
            for dst, src in small:
                sp.dma_start(dst, src, allow_slow_non_contiguous=True).then_inc(s_w["small"], 16)
            sp.wait_ge(s_gclear, 1)
            late = [(nat["wi"][:, :, :], wi.rearrange("(m p) d -> p m d", p=P)),
                    (nat["wo"][:, :, :], wo.rearrange("(m p) f -> p m f", p=P)),
                    (nat["la"][:, 0, :], lora_A.rearrange("e r d -> (e r) d")),
                    (nat["gw"][0:EX, 0, :], gate_w)]
            late += [(nat["lb"][:, :, e, :], lora_B[e].rearrange("(m p) r -> p m r", p=P)) for e in range(EX)]
            for dst, src in late:
                sp.dma_start(dst, src).then_inc(s_w["late"], 16)
            assert (len(loads), len(small), len(late)) == (N_EARLY, N_SMALL, N_LATE)
            sp.wait_ge(s_foldlo, 3)
            sp.wait_ge(s_wlo, len(jobs))

            def load_x(u):
                if u.has(2):
                    sp.wait_ge(ln_norm, nth(u, 1, -1, 0))
                apart(sp)
                sp.dma_start(xin[:, u.slot], x_t[u.index]).then_inc(ln_in[u.slot], 16)

            def store_qkv(u):
                sp.wait_ge(a_fin, nth(u, 2 * 3, 6))
                sp.wait_ge(a_vcopy, nth(u, 1, 1))
                for s in range(3):
                    sp.dma_start(tiles(qkv_d[s])[u.index],
                                 a_out[:, u.slot, :, s * D:(s + 1) * D]).then_inc(a_stored[u.slot], 16)

            over_units(sp, UNITS, [(0, load_x), (2, store_qkv)])
            for i in range(2):
                sp.wait_ge(a_stored[i], 3 * SLOT_FULL)

            def regroup(u, s):
                return qkv_d[s, u.index].rearrange("(g t) (h e) -> t h g e", t=GT, e=HD)

            def load_kv(u):
                if u.has(2):
                    sp.wait_ge(h_part["k"][3], nth(u, 1, -1))
                    sp.wait_ge(h_part["v"][3], nth(u, 1, -1))
                apart(sp)
                for dst, s, landing in ((h_k, 1, h_kin), (h_v, 2, h_vin)):
                    sp.dma_start(dst[:, u.slot].rearrange("p (g e) -> p g e", e=HD), regroup(u, s)).then_inc(landing[u.slot], 16)

            def load_q(u):
                if u.has(2):
                    sp.wait_ge(h_part["q"][3], nth(u, 1, -1))
                apart(sp)
                sp.dma_start(h_q[:, u.slot].rearrange("p (g e) -> p g e", e=HD), regroup(u, 0)).then_inc(h_qin[u.slot], 16)

            def store_w(u):
                sp.wait_ge(h_wd, nth(u, 1, 1))
                apart(sp)
                sp.dma_start(w_d[u.index].rearrange("(g t) (h e) -> t h g e", t=GT, e=HD),
                             h_w[:, :].rearrange("p (g e) -> p g e", e=HD)).then_inc(stored[u.slot], 16)

            def spread_k(u):
                sp.wait_ge(h_part["k"][3], nth(u, 1, 1))
                if u.has(2):
                    apart(sp)
                    sp.wait_ge(h_kv, nth(u, 1, -1))
                apart(sp)
                for t in range(GT):
                    rows = slice(t * H, (t + 1) * H)
                    sp.dma_start(h_kd[rows, u.slot, :, t, :], h_kp[rows]).then_inc(h_kdd[u.slot], 16)

            sp.wait_ge(h_zeroed, 4)
            over_units(sp, UNITS, [(0, load_kv), (0, load_q), (1, spread_k), (4, store_w)])
            for i in range(2):
                sp.wait_ge(stored[i], 1 * SLOT_FULL)

            def load_w(u):
                if u.has(2):
                    sp.wait_ge(m_n1d, nth(u, 1, -1))
                apart(sp)
                sp.dma_start(m_w[:, u.slot], tiles(w_d)[u.index]).then_inc(m_win[u.slot], 16)

            def load_mx(u):
                if u.has(2):
                    sp.wait_ge(m_xad, nth(u, 1, -1))
                apart(sp)
                sp.dma_start(m_x[:, u.slot], x_t[u.index]).then_inc(m_xin[u.slot], 16)

            def store_x1(u):
                sp.wait_ge(m_yd, nth(u, 1, 1))
                apart(sp)
                sp.dma_start(x1_t[u.index], m_y[:, u.slot]).then_inc(stored[u.slot], 16)

            over_units(sp, UNITS, [(0, load_w), (2, load_mx), (4, store_x1)])
            for i in range(2):
                sp.wait_ge(stored[i], 2 * SLOT_FULL)

            def load_xc(u):
                if u.has(2):
                    sp.wait_ge(c_xbd, nth(u, 1, -1))
                    apart(sp)
                    sp.wait_ge(ln_norm, nth(u, 1, -1, 1))
                    apart(sp)
                    sp.wait_ge(c_cnlo, nth(u, 1, -1))
                    apart(sp)
                    sp.wait_ge(c_cturned, nth(u, 1, -1))
                apart(sp)
                sp.dma_start(c_x[:, u.slot], x1_t[u.index]).then_inc(ln_in[u.slot], 16)
                sp.dma_start(c_c[:, u.slot], ctx_t[u.index]).then_inc(c_cin[u.slot], 16)

            def store_x2(u):
                sp.wait_ge(c_yd, nth(u, 2, 2))
                apart(sp)
                sp.dma_start(x2_t[u.index], c_y[:, u.slot]).then_inc(stored[u.slot], 16)

            over_units(sp, UNITS, [(0, load_xc), (2, store_x2)])
            for i in range(2):
                sp.wait_ge(stored[i], 3 * SLOT_FULL)

            sp.dma_start(borow[:, :], bo.rearrange("(a n) -> a n", a=1).broadcast_to([P, D])).then_inc(s_w["small"], 16)

            def load_x2(u):
                if u.has(2):
                    sp.wait_ge(ln_norm, nth(u, 1, -1, 2))
                    apart(sp)
                    sp.wait_ge(f_xbd, nth(u, 1, -1))
                apart(sp)
                sp.dma_start(f_x[:, u.slot], x2_t[u.index]).then_inc(ln_in[u.slot], 16)

            def store_out(u):
                sp.wait_ge(f_yd, nth(u, 2, 2))
                apart(sp)
                sp.dma_start(out_t[u.index], f_y[:, u.slot]).then_inc(stored[u.slot], 16)

            over_units(sp, UNITS, [(0, load_x2), (4, store_out)])
            for i in range(2):
                sp.wait_ge(stored[i], 4 * SLOT_FULL)

        def product(pe, acc, left, right, first=True, last=True, skip=False):
            for n, (a, b) in enumerate(((1, 0), (0, 1), (0, 0))):
                ins = pe.matmul(acc, left(a), right(b), start=first and n == 0, stop=last and n == 2,
                                skip_group_check=skip)
            return ins

        @block.tensor
        def _(pe):
            pe.wait_ge(s_const, 1)
            pe.wait_ge(s_w["early"], 16 * N_EARLY)
            for n, (blks, _, _, _) in enumerate(jobs):
                if n == EARLY:
                    pe.wait_ge(s_w["late"], 16 * N_LATE)
                if n >= 4:
                    pe.wait_ge(s_stage, n - 3)
                for i, b in enumerate(blks):
                    ins = pe.transpose(bank[n % 4][:, i * P:(i + 1) * P], b, identf[:, :])
                ins.then_inc(s_turn, 1)
            for k in range(2):
                for m in range(2):
                    pe.transpose(bank[4][:, k * D + m * P:k * D + (m + 1) * P],
                                 nat["xq"][:, m, k * P:(k + 1) * P], identf[:, :])
            for k in range(2):
                ins = pe.transpose(bank[5][:, k * C:(k + 1) * C], nat["xk"][:, 0, k * P:(k + 1) * P], identf[:, :])
            ins.then_inc(s_fold, 1)
            pe.wait_ge(s_foldc, 2)
            pe.wait_ge(s_small, 2)
            for m in range(KD):
                for k in range(2):
                    pe.matmul(bank[6][:, m * C:(m + 1) * C], xqT[:, k, m * P:(m + 1) * P], xkT[:, k, :],
                              start=k == 0, stop=k == 1)
            for k in range(2):
                pe.matmul(bank[7][:, 0:D], bkwide[:, k, :], xqT[:, k, :], start=k == 0, stop=k == 1)
            for k in range(2):
                pe.matmul(bank[7][:, D:D + 1], bkwide[:, k, :], bqc[:, k:k + 1], start=k == 0, stop=k == 1)
            for k in range(2):
                ins = pe.matmul(bank[7][:, D + 8:D + 9], xkT[:, k, :], bqc[:, k:k + 1], start=k == 0, stop=k == 1)
            ins.then_inc(s_foldm, 1)
            pe.wait_ge(s_folde, 4)
            pe.wait_ge(s_stage, len(jobs))

            def turn(dst, tile):
                for k in range(KD):
                    for i in range(TT):
                        ins = pe.transpose(dst[:, k * T + i * P:k * T + (i + 1) * P],
                                           tile[:, i, k * P:(k + 1) * P], identf[:, :])
                return ins

            def turn_x(u):
                pe.wait_ge(ln_norm, nth(u, 1, 1, 0))
                if u.has(2):
                    pe.wait_ge(ln_lo, nth(u, 1, -1, 0))
                turn(bank[4 * u.slot], a_xn[:, u.slot]).then_inc(ln_turned, 1)

            def project(u):
                pe.wait_ge(ln_lo, nth(u, 1, 1, 0))
                pe.wait_ge(s_wlo, len(jobs))
                if u.has(2):
                    pe.wait_ge(a_elud, nth(u, 2, -2))
                    pe.wait_ge(a_vcopy, nth(u, 1, -1))
                xT = a_xT[u.slot]
                for i in range(TT):
                    for k in range(KD):
                        ins = product(pe, bank[4 * u.slot + 1 + i][:, :],
                                      lambda p: xT[p][:, k, i * P:(i + 1) * P],
                                      lambda p: wqkvT[p][:, k, 0:512], k == 0, k == KD - 1)
                    ins.then_inc(a_qk, 1)
                for i in range(TT):
                    for k in range(KD):
                        ins = product(pe, bank[4 * u.slot + 3][:, i * D:(i + 1) * D],
                                      lambda p: xT[p][:, k, i * P:(i + 1) * P],
                                      lambda p: wqkvT[p][:, k, 512:768], k == 0, k == KD - 1)
                ins.then_inc(a_v, 1)

            over_units(pe, UNITS, [(2, project), (1, turn_x)])
            pe.wait_ge(a_elud, 2 * UNITS)
            pe.wait_ge(a_vcopy, UNITS)

            PAIRS = [(2, 0), (0, 2), (1, 1), (1, 0), (0, 1), (0, 0)]

            def grouped(acc, wide, parts):
                for g in range(GROUPS):
                    for n, (a, b) in enumerate(PAIRS):
                        ins = pe.matmul(acc[:, g * HD:(g + 1) * HD],
                                        wide[:, a].rearrange("p t c -> p (t c)")[:, g:GT * 512:GROUPS],
                                        parts[:, b, g * HD:(g + 1) * HD],
                                        start=n == 0, stop=n == len(PAIRS) - 1)
                return ins

            def heads_kv(u):
                pe.wait_ge(h_kdd[u.slot], landed(u, GT))
                pe.wait_ge(h_part["v"][3], nth(u, 1, 1))
                if u.has(2):
                    pe.wait_ge(h_part["m"][1], nth(u, 1, -1))
                grouped(bank[u.slot], h_kd[:, u.slot], h_vp[:, u.slot]).then_inc(h_kv, 1)

            def heads_out(u):
                pe.wait_ge(h_qdd, nth(u, 3, 3))
                pe.wait_ge(h_part["m"][3], nth(u, 1, 1))
                if u.has(2):
                    pe.wait_ge(h_wd, nth(u, 1, -1))
                grouped(bank[2 + u.slot], h_qd[:, u.slot], h_mp[:, u.slot]).then_inc(h_out, 1)

            over_units(pe, UNITS, [(2, heads_kv), (3, heads_out)])
            pe.wait_ge(h_wd, UNITS)

            def turn_attn(u):
                pe.wait_ge(m_a2d, nth(u, 1, 1))
                if u.has(2):
                    pe.wait_ge(m_lo, nth(u, 1, -1))
                turn(bank[u.slot], m_a2[:, u.slot]).then_inc(m_turned, 1)

            def hidden(u):
                pe.wait_ge(m_lo, nth(u, 1, 1))
                if u.has(2):
                    pe.wait_ge(m_gelu, nth(u, 1, -1))
                for f in range(KD):
                    for k in range(KD):
                        ins = product(pe, bank[2 + u.slot][:, f * T:(f + 1) * T],
                                      lambda p: w1T[p][:, k, f * P:(f + 1) * P],
                                      lambda p: m_aT[u.slot][p][:, k, :], k == 0, k == KD - 1)
                ins.then_inc(m_h, 1)

            def mixed(u):
                pe.wait_ge(m_glo, nth(u, 1, 1))
                if u.has(2):
                    pe.wait_ge(m_yd, nth(u, 1, -1))
                for i in range(TT):
                    for k in range(KD):
                        ins = product(pe, bank[4 + u.slot][:, i * D:(i + 1) * D],
                                      lambda p: m_hT[u.slot][p][:, k, i * P:(i + 1) * P],
                                      lambda p: w2T[p][:, k, :], k == 0, k == KD - 1)
                ins.then_inc(m_o, 1)

            over_units(pe, UNITS, [(4, hidden), (3, turn_attn), (4, mixed)])
            pe.wait_ge(m_yd, UNITS)

            def turn_cx(u):
                pe.wait_ge(c_cin[u.slot], landed(u))
                if u.has(1):
                    pe.wait_ge(c_clo, nth(u, 1, 0))
                for i in range(TT):
                    ins = pe.transpose(bank[1][:, i * P:(i + 1) * P], c_c[:, u.slot, i, :], identf[:, :])
                ins.then_inc(c_cturned, 1)
                pe.wait_ge(ln_norm, nth(u, 1, 1, 1))
                if u.has(1):
                    pe.wait_ge(ln_lo, nth(u, 1, 0, 1))
                turn(bank[0], c_xn[:, u.slot]).then_inc(ln_turned, 1)

            def queries(u):
                pe.wait_ge(ln_lo, nth(u, 1, 1, 1))
                if u.has(1):
                    pe.wait_ge(c_ulo, nth(u, 1, 0))
                for k in range(KD):
                    ins = product(pe, bank[2][:, 0:T], lambda p: mT[p][:, k, :],
                                  lambda p: c_xT[u.slot][p][:, k, :], k == 0, k == KD - 1)
                ins.then_inc(c_u, 1)

            def scores(u):
                pe.wait_ge(c_ulo, nth(u, 1, 1))
                pe.wait_ge(c_clo, nth(u, 1, 1))
                if u.has(1):
                    pe.wait_ge(c_pd, nth(u, 2, 0))
                for i in range(TT):
                    ins = product(pe, bank[3][:, i * T:(i + 1) * T],
                                  lambda p: c_uT[u.slot][p][:, i * P:(i + 1) * P],
                                  lambda p: c_cT[u.slot][p][:, :])
                ins.then_inc(c_s, 1)

            def turn_p(u):
                pe.wait_ge(c_pd, nth(u, 2, 2))
                if u.has(1):
                    pe.wait_ge(c_plo, nth(u, 1, 0))
                turn(bank[4], c_p).then_inc(c_pturned, 1)

            def value(u):
                pe.wait_ge(c_plo, nth(u, 1, 1))
                pe.wait_ge(c_cnlo, nth(u, 1, 1))
                if u.has(1):
                    pe.wait_ge(c_olo, nth(u, 1, 0))
                for k in range(TT):
                    ins = product(pe, bank[5][:, 0:T], lambda p: c_ch[u.slot][p][:, k, :],
                                  lambda p: c_pT[p][:, k, :], k == 0, k == TT - 1)
                ins.then_inc(c_o, 1)

            def crossed(u):
                pe.wait_ge(c_olo, nth(u, 1, 1))
                if u.has(2):
                    pe.wait_ge(c_yd, nth(u, 2, -2))
                for i in range(TT):
                    ins = product(pe, bank[6 + u.slot][:, i * D:(i + 1) * D],
                                  lambda p: c_oT[p][:, i * P:(i + 1) * P], lambda p: xwv[p][:, :])
                ins.then_inc(c_f, 1)

            over_units(pe, UNITS, [(2, scores), (1, turn_cx), (2, turn_p), (2, value), (1, queries), (2, crossed)])
            pe.wait_ge(c_yd, 2 * UNITS)

            def turn_f(u):
                pe.wait_ge(ln_norm, nth(u, 1, 1, 2))
                if u.has(1):
                    pe.wait_ge(ln_lo, nth(u, 1, 0, 2))
                turn(bank[0], f_xn[:, u.slot]).then_inc(ln_turned, 1)

            def adapters_in(u):
                pe.wait_ge(ln_lo, nth(u, 1, 1, 2))
                if u.has(1):
                    pe.wait_ge(f_ad_, nth(u, 1, 0))
                    pe.wait_ge(f_top1, nth(u, 1, 0))
                for n, w in enumerate((gwT, laT)):
                    for k in range(KD):
                        ins = product(pe, bank[1][:, n * T:(n + 1) * T], lambda p: w[p][:, k, :],
                                      lambda p: f_xT[u.slot][p][:, k, :], k == 0, k == KD - 1)
                ins.then_inc(f_la, 1)

            def turn_logits(u):
                pe.wait_ge(f_lTd, nth(u, 1, 1))
                pe.wait_ge(f_ad_, nth(u, 1, 1))
                for i in range(TT):
                    ins = pe.transpose(bank[1][:, i * P:(i + 1) * P], f_lT[:, i * P:(i + 1) * P], identf[:, :])
                ins.then_inc(f_lturned, 1)

            def turn_masks(u):
                pe.wait_ge(f_md, nth(u, 2, 2))
                if u.has(1):
                    pe.wait_ge(f_adm, nth(u, 3, 0))
                for m in range(2):
                    for i in range(TT):
                        ins = pe.matmul(bank[2][:, m * T + i * P:m * T + (i + 1) * P],
                                        f_m[:, m, i].rearrange("p e r -> p (e r)"), identb[:, :],
                                        start=True, stop=True)
                ins.then_inc(f_mT, 1)

            def hidden_first(u, j):
                if j == 0:
                    pe.wait_ge(f_adlo, nth(u, 1, 1))
                if u.has(1):
                    pe.wait_ge(f_h2d, nth(u, 4, j - 3))
                for c in range(2):
                    f = 2 * j + c
                    acc = bank[4 + j][:, c * T:(c + 1) * T]
                    for k in range(KD):
                        product(pe, acc, lambda p: wiT[p][:, k, f * P:(f + 1) * P],
                                lambda p: f_xT[u.slot][p][:, k, :], c == 0 and k == 0, False, True)
                    ins = product(pe, acc, lambda p: lbT[p][:, f * P:(f + 1) * P],
                                  lambda p: f_adT[u.slot][p][:, 0, :], False, False, True)
                ins.then_inc(f_base, 1)

            def hidden_second(u, j):
                pe.wait_ge(f_h1d, nth(u, 4, j + 1))
                for c in range(2):
                    f = 2 * j + c
                    ins = product(pe, bank[4 + j][:, c * T:(c + 1) * T],
                                  lambda p: lbT[p][:, f * P:(f + 1) * P],
                                  lambda p: f_adT[u.slot][p][:, 1, :], False, True, True)
                ins.then_inc(f_more, 1)

            def hidden_a(u):
                hidden_first(u, 0)
                hidden_first(u, 1)
                hidden_second(u, 0)

            def hidden_b(u):
                hidden_first(u, 2)
                hidden_second(u, 1)
                hidden_first(u, 3)
                hidden_second(u, 2)
                hidden_second(u, 3)

            def fed(i):
                def emit(u):
                    if i == 0:
                        pe.wait_ge(f_hlo, nth(u, 4, 4))
                    if i or u.has(1):
                        pe.wait_ge(f_yd, nth(u, 2, i))
                    for f in range(FT):
                        ins = product(pe, bank[3][:, i * D:(i + 1) * D],
                                      lambda p: f_hT[u.slot][p][:, f, i * P:(i + 1) * P],
                                      lambda p: woT[p][:, f, :], f == 0, f == FT - 1)
                    ins.then_inc(f_o, 1)
                return emit

            over_units(pe, UNITS, [(2, adapters_in), (3, hidden_a), (2, turn_logits), (4, fed(0)),
                                   (3, hidden_b), (2, turn_masks), (1, turn_f), (4, fed(1))])

        @block.scalar
        def _(act):
            act.wait_ge(s_w["small"], 16 * N_SMALL)
            for n, (blks, _, _, k) in enumerate(jobs):
                width = len(blks) * P
                act.wait_ge(s_turn, n + 1)
                if n >= 2:
                    act.wait_ge(s_wlo, n - 1)
                act.activation(stage[:, n % 2, 0:width], bank[n % 4][:, 0:width], ACT.Copy,
                               scale=g1c[:, k:k + 1] if k is not None else 1.0).then_inc(s_stage, 1)
            act.wait_ge(s_fold, 1)
            act.activation(flat(xqT[:, :, :]), bank[4][:, :], ACT.Copy).then_inc(s_foldc, 1)
            act.activation(flat(xkT[:, :, :]), bank[5][:, 0:2 * C], ACT.Copy).then_inc(s_foldc, 1)
            act.wait_ge(s_lam, 1)
            act.activation(lexp[:, :], lprod[:, :], ACT.Exp).then_inc(s_lamexp, 1)
            act.wait_ge(s_foldm, 1)
            act.activation(flat(mT[0][:, :, :]), bank[6][:, 0:2 * C], ACT.Copy).then_inc(s_folde, 1)
            act.activation(wbkrow[:, :], bank[7][:, 0:D], ACT.Copy).then_inc(s_folde, 1)
            act.activation(bqbk[:, :], bank[7][:, D:D + 1], ACT.Copy).then_inc(s_folde, 1)
            act.activation(bqk[:, :], bank[7][:, D + 8:D + 9], ACT.Copy).then_inc(s_folde, 1)
            act.activation(xwv[0][:, :], nat["xv"][:, 0, :], ACT.Copy).then_inc(s_folde, 1)
            act.wait_ge(s_foldlo, 3)
            act.wait_ge(s_wlo, len(jobs))

            def a_split(u):
                act.wait_ge(ln_turned, nth(u, 1, 1, 0))
                if u.has(2):
                    act.wait_ge(a_v, nth(u, 1, -1))
                act.activation(flat(a_xT[u.slot][0][:, :, :]), bank[4 * u.slot][:, :], ACT.Copy).then_inc(ln_hi, 1)

            def a_exps(u):
                for i in range(TT):
                    b = bank[4 * u.slot + 1 + i]
                    act.wait_ge(a_qk, nth(u, 2, i + 1))
                    if u.has(1):
                        act.wait_ge(a_elud, nth(u, 2, i - 1))
                    act.activation(a_exp[:, i], b[:, :], ACT.Relu, scale=-1.0).then_inc(a_negd, 1)
                    act.wait_ge(a_negd, nth(u, 2, i + 1))
                    act.activation(a_exp[:, i], a_exp[:, i], ACT.Exp, scale=-1.0).then_inc(a_expd, 1)
                act.wait_ge(a_v, nth(u, 1, 1))
                if u.has(2):
                    act.wait_ge(a_stored[u.slot], u.turn * 48)
                act.activation(a_out[:, u.slot, :, 2 * D:3 * D],
                               bank[4 * u.slot + 3][:, :].rearrange("p (i d) -> p i d", i=TT),
                               ACT.Copy).then_inc(a_vcopy, 1)

            over_units(act, UNITS, [(2, a_exps), (1, a_split)])
            for i in range(2):
                act.wait_ge(a_stored[i], 3 * SLOT_FULL)

            def part1(key, dst, src):
                act.activation(dst, src, ACT.Copy).then_inc(h_part[key][0], 1)

            def part2(u, key, dst, r):
                act.wait_ge(h_part[key][1], nth(u, 1, 1))
                act.activation(dst[:, 1], h_r[:, r], ACT.Copy).then_inc(h_part[key][2], 1)

            def kv_parts(u):
                act.wait_ge(h_kin[u.slot], landed(u))
                if u.has(1):
                    act.wait_ge(h_kdd[u.before(1).slot], landed(u.before(1), GT))
                part1("k", in_e(h_kp[:, 0]), by_e(h_k[:, u.slot]))

            def kv_rest(u):
                act.wait_ge(h_vin[u.slot], landed(u))
                if u.has(2):
                    act.wait_ge(h_kv, nth(u, 1, -1))
                part1("v", h_vp[:, u.slot, 0], h_v[:, u.slot])
                part2(u, "k", h_kp, 0)
                part2(u, "v", h_vp[:, u.slot], 1)

            def q_parts(u):
                act.wait_ge(h_qin[u.slot], landed(u))
                if u.has(1):
                    act.wait_ge(h_qdd, nth(u, 3, 0))
                part1("q", in_e(h_qp[:, 0]), by_e(h_q[:, u.slot]))

            def q_second(u):
                part2(u, "q", h_qp, 1)

            def m_parts(u):
                act.wait_ge(h_kv, nth(u, 1, 1))
                if u.has(2):
                    act.wait_ge(h_out, nth(u, 1, -1))
                part1("m", h_mp[:, u.slot, 0], bank[u.slot][:, :])
                part2(u, "m", h_mp[:, u.slot], 2)

            def w_copy(u):
                act.wait_ge(h_out, nth(u, 1, 1))
                if u.has(1):
                    act.wait_ge(stored[u.before(1).slot], landed(u.before(1)))
                act.activation(h_w[:, :], bank[2 + u.slot][:, :], ACT.Copy).then_inc(h_wd, 1)

            over_units(act, UNITS, [(2, q_parts), (1, kv_parts), (2, q_second), (1, kv_rest), (4, w_copy), (2, m_parts)])
            for i in range(2):
                act.wait_ge(stored[i], 1 * SLOT_FULL)

            def m_squares(u):
                act.wait_ge(m_win[u.slot], landed(u))
                if u.has(1):
                    act.wait_ge(m_ssd, nth(u, 1, 0))
                act.activation(flat(m_sq[:, :, :]), flat(m_w[:, u.slot]), ACT.Square).then_inc(m_sqd, 1)

            def m_squares3(u):
                act.wait_ge(m_atd, nth(u, 1, 1))
                if u.has(1):
                    act.wait_ge(m_m3d, nth(u, 1, 0))
                    act.wait_ge(m_t3d, nth(u, 2, 0))
                for i in range(TT):
                    act.activation(m_t3[:, i], m_at[:, i], ACT.Square, accum_out=m_s3[:, i:i + 1]).then_inc(m_s3d, 1)

            def m_split(u):
                act.wait_ge(m_turned, nth(u, 1, 1))
                if u.has(2):
                    act.wait_ge(m_h, nth(u, 1, -1))
                act.activation(flat(m_aT[u.slot][0][:, :, :]), bank[u.slot][:, :], ACT.Copy).then_inc(m_hi, 1)

            def m_gelus(u):
                act.wait_ge(m_h, nth(u, 1, 1))
                if u.has(2):
                    act.wait_ge(m_glo, nth(u, 1, -1))
                act.activation(m_g[:, u.slot], bank[2 + u.slot][:, :], ACT.Gelu).then_inc(m_gelu, 1)

            over_units(act, UNITS, [(4, m_gelus), (3, m_split), (2, m_squares3), (0, m_squares)])
            for i in range(2):
                act.wait_ge(stored[i], 2 * SLOT_FULL)

            def c_context(u):
                act.wait_ge(c_cturned, nth(u, 1, 1))
                if u.has(2):
                    act.wait_ge(c_s, nth(u, 1, -1))
                act.activation(c_cT[u.slot][0][:, :], bank[1][:, 0:T], ACT.Copy).then_inc(c_chi, 1)

            def c_split(u):
                act.wait_ge(ln_turned, nth(u, 1, 1, 1))
                if u.has(2):
                    act.wait_ge(c_u, nth(u, 1, -1))
                act.activation(flat(c_xT[u.slot][0][:, :, :]), bank[0][:, :], ACT.Copy).then_inc(ln_hi, 1)

            def c_exps(u):
                act.wait_ge(c_nbd, nth(u, 1, 1))
                if u.has(1):
                    act.wait_ge(c_pturned, nth(u, 1, 0))
                    act.wait_ge(c_invd, nth(u, 1, 0))
                for i in range(TT):
                    act.activation(c_p[:, i], bank[3][:, i * T:(i + 1) * T], ACT.Exp, bias=c_nb[:, i:i + 1],
                                   accum_out=c_sum[:, i:i + 1]).then_inc(c_pd, 1)

            def c_psplit(u):
                act.wait_ge(c_pturned, nth(u, 1, 1))
                if u.has(1):
                    act.wait_ge(c_o, nth(u, 1, 0))
                act.activation(flat(c_pT[0][:, :, :]), bank[4][:, :], ACT.Copy).then_inc(c_phi, 1)

            def c_osplit(u):
                act.wait_ge(c_o, nth(u, 1, 1))
                if u.has(1):
                    act.wait_ge(c_f, nth(u, 1, 0))
                act.activation(c_oT[0][:, :], bank[5][:, 0:T], ACT.Copy).then_inc(c_ohi, 1)

            over_units(act, UNITS, [(1, c_context), (2, c_exps), (1, c_split), (2, c_psplit), (2, c_osplit)])
            for i in range(2):
                act.wait_ge(stored[i], 3 * SLOT_FULL)

            def f_split(u):
                act.wait_ge(ln_turned, nth(u, 1, 1, 2))
                if u.has(2):
                    act.wait_ge(f_base, nth(u, 4, -4))
                act.activation(flat(f_xT[u.slot][0][:, :, :]), bank[0][:, :], ACT.Copy).then_inc(ln_hi, 1)

            def f_adapters(u):
                act.wait_ge(f_la, nth(u, 1, 1))
                if u.has(1):
                    act.wait_ge(f_lturned, nth(u, 1, 0))
                act.activation(f_lT[:, :], bank[1][:, 0:T], ACT.Copy).then_inc(f_lTd, 1)
                if u.has(2):
                    act.wait_ge(f_adm, nth(u, 3, -3))
                act.activation(f_a[:, u.slot], bank[1][:, T:2 * T], ACT.Copy).then_inc(f_ad_, 1)

            def f_exps(u):
                act.wait_ge(f_top1, nth(u, 1, 1))
                if u.has(1):
                    act.wait_ge(f_top2, nth(u, 1, 0))
                act.activation(flat(f_ex[:, :, :]), flat(f_sh[:, :, :]), ACT.Exp).then_inc(f_exd, 1)

            def relus(u, j, ready, out_slot, done, back):
                act.wait_ge(ready, nth(u, 4, j + 1))
                if j >= 2 or u.has(1):
                    act.wait_ge(f_hsd, nth(u, 4, j - 1))
                for c in range(2):
                    f = 2 * j + c
                    ins = act.activation(out_slot[:, j % 2, c * T:(c + 1) * T], bank[4 + j][:, c * T:(c + 1) * T],
                                         ACT.Relu, bias=bic[:, f:f + 1])
                ins.then_inc(done, 1)

            def relus_a(u):
                relus(u, 0, f_base, f_h1, f_h1d, 0)
                relus(u, 1, f_base, f_h1, f_h1d, 0)
                relus(u, 0, f_more, f_h2, f_h2d, 0)

            def relus_b(u):
                relus(u, 1, f_more, f_h2, f_h2d, 0)
                relus(u, 2, f_base, f_h1, f_h1d, 0)
                relus(u, 3, f_base, f_h1, f_h1d, 0)
                relus(u, 2, f_more, f_h2, f_h2d, 0)
                relus(u, 3, f_more, f_h2, f_h2d, 0)

            over_units(act, UNITS, [(2, f_adapters), (3, relus_a), (2, f_exps), (3, relus_b), (1, f_split)])

        @block.vector
        def _(dve):
            dve.memset(mhalf[:, :], -0.5)
            dve.memset(nat["gw"][:, 0, :], 0.0).then_inc(s_gclear, 1)
            dve.memset(onesw[:, :], 1.0).then_inc(s_small, 1)
            dve.wait_ge(s_w["small"], 16 * N_SMALL)
            dve.tensor_tensor(lprod[:, :], lamt[:, 0:4:2], lamt[:, 1:4:2], ALU.mult).then_inc(s_lam, 1)
            dve.wait_ge(s_small, 1)
            for k in range(2):
                ins = dve.tensor_scalar(bkwide[:, k, :], onesw[:, :], bkc[:, k:k + 1], None, ALU.mult)
            ins.then_inc(s_small, 1)
            for h in range(H):
                dve.tensor_scalar(g2row[:, h, :], g2raw[:, 0, :], 1.0 - LAMBDA_INIT, None, ALU.mult)
            for n, (blks, dst, at, k) in enumerate(jobs):
                width = len(blks) * P
                dve.wait_ge(s_stage, n + 1)
                dve.tensor_copy(target(dst[0], at), stage[:, n % 2, 0:width]).then_inc(s_whi, 1)
                if n % 2:
                    dve.wait_ge(s_whi, n + 1)
                    dve.wait_ge(s_wlo, n)
                    dve.tensor_tensor(target(dst[1], at), stage[:, n % 2, 0:width],
                                      target(dst[0], at).bitcast(F32), ALU.subtract).then_inc(s_wlo, 1)
            dve.wait_ge(s_lamexp, 1)
            dve.tensor_tensor(ldiff[:, :], lexp[:, 1:2], lexp[:, 0:1], ALU.subtract).then_inc(s_lam, 1)
            dve.wait_ge(s_lam, 2)
            dve.tensor_scalar(qfac[:, :], ldiff[:, :], LAMBDA_INIT, HEAD_SCALE, ALU.subtract, ALU.mult).then_inc(s_foldlo, 1)
            dve.wait_ge(s_folde, 5)
            dve.tensor_tensor(flat(mT[1][:, :, :]), bank[6][:, 0:2 * C], flat(mT[0][:, :, :]).bitcast(F32),
                              ALU.subtract).then_inc(s_foldlo, 1)
            dve.tensor_tensor(xwv[1][:, :], nat["xv"][:, 0, :], xwv[0][:, :].bitcast(F32), ALU.subtract).then_inc(s_foldlo, 1)
            dve.wait_ge(s_foldlo, 3)
            dve.wait_ge(s_wlo, len(jobs))

            def moments(u, loops, src, st, mv):
                dve.wait_ge(ln_in[u.slot], landed(u, 1, loops))
                for i in range(TT):
                    ins = dve.bn_stats(st[:, u.slot, i, :], src[:, u.slot, i, :])
                ins.then_inc(ln_stats, 1)
                dve.wait_ge(ln_stats, nth(u, 1, 1, loops))
                apart(dve)
                for i in range(TT):
                    ins = dve.bn_aggr(mv[:, u.slot, i, :], st[:, u.slot, i, :])
                ins.then_inc(ln_var, 1)

            def normalise(u, loops, src, mv, rs, dst):
                dve.wait_ge(ln_rstd, nth(u, 1, 1, loops))
                for i in range(TT):
                    ins = dve.tensor_scalar(dst[:, u.slot, i, :], src[:, u.slot, i, :], mv[:, u.slot, i, 0:1],
                                            rs[:, u.slot, i:i + 1], ALU.subtract, ALU.mult)
                ins.then_inc(ln_norm, 1)

            def low(u, hi_done, hi, lo, src, done, loops=0):
                dve.wait_ge(hi_done, nth(u, 1, 1, loops))
                dve.tensor_tensor(lo, src, hi.bitcast(F32), ALU.subtract).then_inc(done, 1)

            def a_moments(u):
                moments(u, 0, xin, a_st, a_mv)

            def a_normalise(u):
                if u.has(2):
                    dve.wait_ge(ln_turned, nth(u, 1, -1, 0))
                normalise(u, 0, xin, a_mv, a_rs, a_xn)

            def a_low(u):
                low(u, ln_hi, flat(a_xT[u.slot][0][:, :, :]), flat(a_xT[u.slot][1][:, :, :]),
                    bank[4 * u.slot][:, :], ln_lo)

            def a_elus(u):
                for i in range(TT):
                    dve.wait_ge(a_expd, nth(u, 2, i + 1))
                    if u.has(1):
                        dve.wait_ge(a_fin, nth(u, 6, 3 * i - 3))
                    dve.scalar_tensor_tensor(out=a_elu[:, i], in0=bank[4 * u.slot + 1 + i][:, :], scalar=0.0,
                                             in1=a_exp[:, i], op0=ALU.max, op1=ALU.add).then_inc(a_elud, 1)

            over_units(dve, UNITS, [(1, a_moments), (2, a_elus), (1, a_normalise), (1, a_low)])
            for i in range(2):
                dve.wait_ge(a_stored[i], 3 * SLOT_FULL)

            def rest(u, key, src, dst, r):
                dve.wait_ge(h_part[key][0], nth(u, 1, 1))
                if u.has(1):
                    dve.wait_ge(h_part[key][3], nth(u, 1, 0))
                dve.tensor_tensor(h_r[:, r], src, dst[:, 0], ALU.subtract).then_inc(h_part[key][1], 1)

            def part3(u, key, dst, r):
                dve.wait_ge(h_part[key][2], nth(u, 1, 1))
                dve.tensor_tensor(dst[:, 2], h_r[:, r], dst[:, 1], ALU.subtract).then_inc(h_part[key][3], 1)

            def k_part3(u):
                part3(u, "k", h_kp, 0)

            def q_part3(u):
                part3(u, "q", h_qp, 1)

            def m_rest(u):
                dve.wait_ge(h_kv, nth(u, 1, 1))
                rest(u, "m", bank[u.slot][:, :], h_mp[:, u.slot], 2)

            def m_part3(u):
                part3(u, "m", h_mp[:, u.slot], 2)

            def spread_q(part):
                def emit(u):
                    dve.wait_ge(h_part["q"][(0, 2, 3)[part]], nth(u, 1, 1))
                    if part == 0 and u.has(2):
                        dve.wait_ge(h_out, nth(u, 1, -1))
                    for t in range(GT):
                        ins = dve.tensor_scalar(h_qd[:, u.slot, part, t, :], h_qp[:, part], slotmask[:, t:t + 1],
                                                None, ALU.mult)
                    ins.then_inc(h_qdd, 1)
                return emit

            over_units(dve, UNITS, [(2, spread_q(0)), (2, q_part3), (1, k_part3), (2, spread_q(1)), (2, spread_q(2)),
                                    (2, m_rest), (2, m_part3)])
            for i in range(2):
                dve.wait_ge(stored[i], 1 * SLOT_FULL)

            def m_sums(u):
                dve.wait_ge(m_sqd, nth(u, 1, 1))
                if u.has(1):
                    dve.wait_ge(m_msd, nth(u, 1, 0))
                dve.tensor_reduce(m_ss[:, :], m_sq[:, :, :].rearrange("p i (h e) -> p (i h) e", e=HD),
                                  AX_X, ALU.add).then_inc(m_ssd, 1)

            def m_heads(u):
                dve.wait_ge(m_rhd, nth(u, 1, 1))
                wide = m_rh[:, u.slot].rearrange("p (n o) -> p n o", o=1).broadcast_to([P, TT * H, HD])
                dve.tensor_tensor(m_n1[:, :, :].rearrange("p i (h e) -> p (i h) e", e=HD),
                                  m_w[:, u.slot].rearrange("p i (h e) -> p (i h) e", e=HD), wide, ALU.mult).then_inc(m_n1d, 1)
                dve.wait_ge(m_n1d, nth(u, 1, 1))
                if u.has(1):
                    dve.wait_ge(m_a2d, nth(u, 1, 0))
                for i in range(TT):
                    ins = dve.tensor_tensor(m_at[:, i], m_n1[:, i], g2row[:, :, :].rearrange("p h e -> p (h e)"), ALU.mult)
                ins.then_inc(m_atd, 1)

            def m_third(u):
                dve.wait_ge(m_r3d, nth(u, 1, 1))
                dve.wait_ge(m_s3d, nth(u, 2, 2))
                for i in range(TT):
                    ins = dve.scalar_tensor_tensor(out=m_t3[:, i], in0=m_at[:, i], scalar=m_r3[:, i:i + 1],
                                                   in1=g3row[:, :], op0=ALU.mult, op1=ALU.mult)
                    ins.then_inc(m_t3d, 1)

            def m_sum(u):
                dve.wait_ge(m_t3d, nth(u, 2, 2))
                if u.has(2):
                    dve.wait_ge(m_turned, nth(u, 1, -1))
                dve.tensor_tensor(flat(m_a2[:, u.slot]), flat(m_t3[:, :, :]), flat(m_at[:, :, :]), ALU.add).then_inc(m_a2d, 1)

            def m_with_x(u):
                dve.wait_ge(m_xin[u.slot], landed(u))
                dve.wait_ge(m_a2d, nth(u, 1, 1))
                if u.has(2):
                    dve.wait_ge(m_yd, nth(u, 1, -1))
                dve.tensor_tensor(flat(m_xa[:, u.slot]), flat(m_a2[:, u.slot]), flat(m_x[:, u.slot]), ALU.add).then_inc(m_xad, 1)

            def m_low(u):
                low(u, m_hi, flat(m_aT[u.slot][0][:, :, :]), flat(m_aT[u.slot][1][:, :, :]), bank[u.slot][:, :], m_lo)

            def m_gsplit(u):
                dve.wait_ge(m_gelu, nth(u, 1, 1))
                if u.has(2):
                    dve.wait_ge(m_o, nth(u, 1, -1))
                hi, lo = (flat(m_hT[u.slot][p][:, :, :]) for p in range(2))
                dve.tensor_copy(hi, m_g[:, u.slot]).then_inc(m_ghi, 1)
                dve.wait_ge(m_ghi, nth(u, 1, 1))
                dve.tensor_tensor(lo, m_g[:, u.slot], hi.bitcast(F32), ALU.subtract).then_inc(m_glo, 1)

            def m_residual(u):
                dve.wait_ge(m_o, nth(u, 1, 1))
                dve.wait_ge(m_xad, nth(u, 1, 1))
                if u.has(2):
                    dve.wait_ge(stored[u.slot], u.turn * 16 + 1 * SLOT_FULL)
                dve.tensor_tensor(flat(m_y[:, u.slot]), bank[4 + u.slot][:, :], flat(m_xa[:, u.slot]), ALU.add).then_inc(m_yd, 1)

            over_units(dve, UNITS, [(3, m_third), (3, m_sum), (2, m_heads), (4, m_gsplit), (3, m_low), (3, m_with_x),
                                    (4, m_residual), (0, m_sums)])
            for i in range(2):
                dve.wait_ge(stored[i], 2 * SLOT_FULL)

            def c_moments(u):
                moments(u, 1, c_x, c_st, c_mv)

            def c_normalise(u):
                if u.has(2):
                    dve.wait_ge(ln_turned, nth(u, 1, -1, 1))
                    dve.wait_ge(c_rrd, nth(u, 1, -1))
                normalise(u, 1, c_x, c_mv, c_rs, c_xn)

            def c_constant(u):
                dve.wait_ge(c_rrd, nth(u, 1, 1))
                dve.tensor_reduce(c_r[:, u.slot], c_rr[:, :, :], AX_X, ALU.add).then_inc(c_rd, 1)

            def c_clow(u):
                low(u, c_chi, c_cT[u.slot][0][:, :], c_cT[u.slot][1][:, :], bank[1][:, 0:T], c_clo)

            def c_low(u):
                low(u, ln_hi, flat(c_xT[u.slot][0][:, :, :]), flat(c_xT[u.slot][1][:, :, :]), bank[0][:, :], ln_lo, 1)

            def c_usplit(u):
                dve.wait_ge(c_u, nth(u, 1, 1))
                if u.has(2):
                    dve.wait_ge(c_s, nth(u, 1, -1))
                dve.tensor_scalar(c_uT[u.slot][0][:, :], bank[2][:, 0:T], bqk[:, 0:1], None, ALU.add).then_inc(c_uhi, 1)
                dve.wait_ge(c_uhi, nth(u, 1, 1))
                dve.scalar_tensor_tensor(out=c_uT[u.slot][1][:, :], in0=bank[2][:, 0:T], scalar=bqk[:, 0:1],
                                         in1=c_uT[u.slot][0][:, :].bitcast(F32), op0=ALU.add,
                                         op1=ALU.subtract).then_inc(c_ulo, 1)

            def c_max(u):
                dve.wait_ge(c_s, nth(u, 1, 1))
                dve.tensor_reduce(c_mx[:, :], bank[3][:, :].rearrange("p (i k) -> p i k", i=TT),
                                  AX_X, ALU.max).then_inc(c_mxd, 1)
                dve.wait_ge(c_mxd, nth(u, 1, 1))
                dve.scalar_tensor_tensor(out=c_mr[:, :], in0=c_r[:, u.slot], scalar=bqbk[:, 0:1], in1=c_mx[:, :],
                                         op0=ALU.add, op1=ALU.add).then_inc(c_mrd, 1)
                dve.wait_ge(c_mrd, nth(u, 1, 1))
                if u.has(1):
                    dve.wait_ge(c_pd, nth(u, 2, 0))
                dve.scalar_tensor_tensor(out=c_nb[:, :], in0=c_r[:, u.slot], scalar=bqbk[:, 0:1], in1=c_mr[:, :],
                                         op0=ALU.add, op1=ALU.subtract).then_inc(c_nbd, 1)

            def c_plow(u):
                dve.wait_ge(c_pd, nth(u, 2, 2))
                dve.reciprocal(c_inv[:, :], c_sum[:, :]).then_inc(c_invd, 1)
                low(u, c_phi, flat(c_pT[0][:, :, :]), flat(c_pT[1][:, :, :]), bank[4][:, :], c_plo)

            def c_olow(u):
                low(u, c_ohi, c_oT[0][:, :], c_oT[1][:, :], bank[5][:, 0:T], c_olo)

            def c_residual(u):
                dve.wait_ge(c_f, nth(u, 1, 1))
                dve.wait_ge(c_xbd, nth(u, 1, 1))
                dve.wait_ge(c_invd, nth(u, 1, 1))
                if u.has(2):
                    dve.wait_ge(stored[u.slot], u.turn * 16 + 2 * SLOT_FULL)
                for i in range(TT):
                    dve.scalar_tensor_tensor(out=c_y[:, u.slot, i], in0=bank[6 + u.slot][:, i * D:(i + 1) * D],
                                             scalar=c_inv[:, i:i + 1], in1=c_xb[:, u.slot, i],
                                             op0=ALU.mult, op1=ALU.add).then_inc(c_yd, 1)

            over_units(dve, UNITS, [(1, c_moments), (2, c_max), (1, c_clow), (1, c_normalise), (2, c_plow),
                                    (1, c_low), (2, c_olow), (1, c_usplit), (1, c_constant), (2, c_residual)])
            for i in range(2):
                dve.wait_ge(stored[i], 3 * SLOT_FULL)

            def f_moments(u):
                moments(u, 2, f_x, f_st, f_mv)

            def f_normalise(u):
                if u.has(2):
                    dve.wait_ge(ln_turned, nth(u, 1, -1, 2))
                normalise(u, 2, f_x, f_mv, f_rs, f_xn)

            def f_low(u):
                low(u, ln_hi, flat(f_xT[u.slot][0][:, :, :]), flat(f_xT[u.slot][1][:, :, :]), bank[0][:, :], ln_lo, 2)

            chain = {"n": 0, "sem": f_chain}
            LINKS = 11

            def link(u, ins):
                chain["n"] += 1
                ins.then_inc(chain["sem"], 1)
                dve.wait_ge(chain["sem"], nth(u, LINKS, chain["n"]))

            def f_shift(u):
                chain["n"] = 0
                dve.wait_ge(f_lturned, nth(u, 1, 1))
                link(u, dve.tensor_tensor(f_lg[:, :, :], bank[1][:, 0:TT * P].rearrange("p (i e) -> p i e", i=TT)[:, :, 0:EX],
                                          gbrow[:, :].rearrange("p (o e) -> p o e", o=1).broadcast_to([P, TT, EX]), ALU.add))
                link(u, dve.tensor_reduce(f_mx[:, :], f_lg[:, :, :], AX_X, ALU.max))
                dve.tensor_tensor(f_sh[:, :, :], f_lg[:, :, :],
                                  f_mx[:, :].rearrange("p (i o) -> p i o", o=1).broadcast_to([P, TT, EX]),
                                  ALU.subtract).then_inc(f_top1, 1)

            def f_rank(u):
                dve.wait_ge(f_exd, nth(u, 1, 1))
                link(u, dve.tensor_reduce(f_sm[:, :], f_ex[:, :, :], AX_X, ALU.add))
                link(u, dve.reciprocal(f_iv[:, :], f_sm[:, :]))
                ins = dve.tensor_tensor(f_sc[:, :, :], f_ex[:, :, :],
                                        f_iv[:, :].rearrange("p (i o) -> p i o", o=1).broadcast_to([P, TT, EX]), ALU.mult)
                link(u, ins)
                for i in range(TT):
                    mine = f_sc[:, i, :].rearrange("p (e o) -> p e o", o=1).broadcast_to([P, EX, EX])
                    other = f_sc[:, i, :].rearrange("p (o j) -> p o j", o=1).broadcast_to([P, EX, EX])
                    dve.tensor_tensor(f_gt[:, i], other, mine, ALU.is_gt)
                    ins = dve.tensor_tensor(f_eq[:, i], other, mine, ALU.is_equal)
                link(u, ins)
                for i in range(TT):
                    ins = dve.tensor_tensor(f_eq[:, i], f_eq[:, i], tril[:, :, :], ALU.mult)
                link(u, ins)
                link(u, dve.tensor_tensor(f_gt[:, :, :, :].rearrange("p i e j -> p (i e j)"),
                                          f_gt[:, :, :, :].rearrange("p i e j -> p (i e j)"),
                                          f_eq[:, :, :, :].rearrange("p i e j -> p (i e j)"), ALU.add))
                link(u, dve.tensor_reduce(f_rk[:, :, :].rearrange("p i e -> p (i e)"),
                                          f_gt[:, :, :, :].rearrange("p i e j -> p (i e) j"), AX_X, ALU.add))
                if u.has(1):
                    dve.wait_ge(f_mT, nth(u, 1, 0))
                for m in range(2):
                    for i in range(TT):
                        ins = dve.tensor_scalar(f_m[:, m, i],
                                                f_rk[:, i, :].rearrange("p (e o) -> p e o", o=1).broadcast_to([P, EX, R]),
                                                float(m), None, ALU.is_equal)
                    ins.then_inc(f_md, 1)
                link(u, dve.scalar_tensor_tensor(out=flat(f_top[:, :, :]), in0=flat(f_rk[:, :, :]), scalar=1.5,
                                                 in1=flat(f_sc[:, :, :]), op0=ALU.is_lt, op1=ALU.mult))
                ins = dve.tensor_reduce(f_vs[:, u.slot], f_top[:, :, :], AX_X, ALU.add)
                ins.then_inc(f_vsd, 1)
                dve.wait_ge(f_vsd, nth(u, 1, 1))
                if u.has(1):
                    dve.wait_ge(f_bod, nth(u, 1, 0))
                link(u, dve.tensor_scalar(f_vs2[:, :], f_vs[:, u.slot], 2.0, None, ALU.mult))
                assert chain["n"] == LINKS
                dve.memset(f_iv[:, 0:1], 0.0).then_inc(f_top2, 1)

            def f_masked(u):
                dve.wait_ge(f_mT, nth(u, 1, 1))
                dve.wait_ge(f_ad_, nth(u, 1, 1))
                if u.has(1):
                    dve.wait_ge(f_adlo, nth(u, 1, 0))
                for m in range(2):
                    dve.tensor_tensor(f_ad[:, m], f_a[:, u.slot], bank[2][:, m * T:(m + 1) * T], ALU.mult).then_inc(f_adm, 1)
                dve.wait_ge(f_adm, nth(u, 3, 2))
                dve.tensor_tensor(f_ad[:, 1], f_ad[:, 1], f_ad[:, 0], ALU.subtract).then_inc(f_adm, 1)
                dve.wait_ge(f_adm, nth(u, 3, 3))
                if u.has(2):
                    dve.wait_ge(f_more, nth(u, 4, -4))
                hi, lo = (flat(f_adT[u.slot][p][:, :, :]) for p in range(2))
                dve.tensor_copy(hi, flat(f_ad[:, :, :])).then_inc(f_adhi, 1)
                dve.wait_ge(f_adhi, nth(u, 1, 1))
                dve.tensor_tensor(lo, flat(f_ad[:, :, :]), hi.bitcast(F32), ALU.subtract).then_inc(f_adlo, 1)

            def hidden_split(j):
                def emit(u):
                    dve.wait_ge(f_hsd, nth(u, 4, j + 1))
                    if j == 0 and u.has(2):
                        dve.wait_ge(f_o, nth(u, 2, -2))
                    hi, lo = (flat(f_hT[u.slot][p][:, 2 * j:2 * j + 2, :]) for p in range(2))
                    dve.tensor_copy(hi, f_hs[:, j % 2]).then_inc(f_hhi, 1)
                    dve.wait_ge(f_hhi, nth(u, 4, j + 1))
                    dve.tensor_tensor(lo, f_hs[:, j % 2], hi.bitcast(F32), ALU.subtract).then_inc(f_hlo, 1)
                return emit

            def f_keep(u):
                if u.has(2):
                    dve.wait_ge(f_yd, nth(u, 2, -2))
                dve.tensor_copy(f_vk[:, u.slot], f_vs[:, u.slot]).then_inc(f_vkd, 1)

            def f_residual(i):
                def emit(u):
                    dve.wait_ge(f_vkd, nth(u, 1, 1))
                    dve.wait_ge(f_o, nth(u, 2, i + 1))
                    if i == 0:
                        dve.wait_ge(f_xbd, nth(u, 1, 1))
                        if u.has(2):
                            dve.wait_ge(stored[u.slot], u.turn * 16 + 3 * SLOT_FULL)
                    dve.scalar_tensor_tensor(out=f_y[:, u.slot, i], in0=bank[3][:, i * D:(i + 1) * D],
                                             scalar=f_vk[:, u.slot, i:i + 1], in1=f_xb[:, u.slot, i],
                                             op0=ALU.mult, op1=ALU.add).then_inc(f_yd, 1)
                return emit

            over_units(dve, UNITS, [(1, f_moments), (3, f_keep), (2, f_shift), (3, hidden_split(0)), (1, f_normalise),
                                    (4, f_residual(0)), (2, f_rank),
                                    (3, hidden_split(1)), (3, hidden_split(2)), (2, f_masked), (3, hidden_split(3)),
                                    (1, f_low), (4, f_residual(1))])

        @block.gpsimd
        def _(pool):
            pool.memset(identf[:, :], 0.0).then_inc(s_cleared, 1)
            pool.memset(tril[:, :, :], 1.0).then_inc(s_cleared, 1)
            pool.memset(slotmask[:, :], 1.0).then_inc(s_cleared, 1)
            pool.wait_ge(s_cleared, 3)
            pool.affine_select(out=identf[:, :], in_=identf[:, :], compare_op=ALU.not_equal, fill=1.0, base=0,
                               pattern=[[-1, P]], channel_multiplier=1).then_inc(s_const, 1)
            pool.affine_select(out=tril[:, :, :], in_=tril[:, :, :], compare_op=ALU.is_gt, fill=0.0, base=0,
                               pattern=[[1, EX], [-1, EX]], channel_multiplier=0)
            pool.affine_select(out=slotmask[:, :], in_=slotmask[:, :], compare_op=ALU.is_ge, fill=0.0, base=0,
                               pattern=[[-H, GT]], channel_multiplier=1).then_inc(s_cleared, 1)
            pool.wait_ge(s_cleared, 4)
            pool.affine_select(out=slotmask[:, :], in_=slotmask[:, :], compare_op=ALU.is_gt, fill=0.0, base=H,
                               pattern=[[H, GT]], channel_multiplier=-1)
            pool.wait_ge(s_const, 1)
            pool.tensor_copy(identb[:, :], identf[:, :])
            for n, (blks, dst, at, k) in enumerate(jobs):
                if n % 2 == 0:
                    width = len(blks) * P
                    pool.wait_ge(s_whi, n + 1)
                    if n:
                        pool.wait_ge(s_wlo, n)
                    pool.tensor_tensor(target(dst[1], at), stage[:, n % 2, 0:width],
                                       target(dst[0], at).bitcast(F32), ALU.subtract).then_inc(s_wlo, 1)
            pool.wait_ge(s_foldlo, 3)
            pool.wait_ge(s_wlo, len(jobs))

            def rstd(u, step_sem, ready, src, scale, add, tmp, out_ap, width, done, loops=0):
                pool.wait_ge(*ready)
                apart(pool)
                pool.tensor_scalar(tmp, src, scale, add, ALU.mult, ALU.add).then_inc(step_sem, 1)
                pool.wait_ge(step_sem, nth(u, 1, 1, loops))
                pool.tensor_tensor(out_ap, tmp, mhalf[:, 0:width], ALU.pow).then_inc(done, 1)


            def a_rstds(u):
                if u.has(2):
                    pool.wait_ge(ln_norm, nth(u, 1, -1, 0))
                rstd(u, ln_ved, (ln_var, nth(u, 1, 1, 0)), a_mv[:, u.slot, :, 1], 1.0 + RMS_EPS, RMS_EPS * LN_EPS,
                     a_ve[:, u.slot], a_rs[:, u.slot], TT, ln_rstd, 0)

            def a_final(u):
                for i in range(TT):
                    pool.wait_ge(a_elud, nth(u, 2, i + 1))
                    if i == 0 and u.has(2):
                        pool.wait_ge(a_stored[u.slot], u.turn * 48)
                    apart(pool)
                    for lo, hi, fac in ((0, P, HEAD_SCALE), (P, D, qfac[:, 0:1]), (D, 2 * D, 1.0)):
                        pool.tensor_scalar(a_out[:, u.slot, i, lo:hi], a_elu[:, i, lo:hi], -1.0, fac,
                                           ALU.add, ALU.mult).then_inc(a_fin, 1)

            wide_flat = h_kd[:, :, :, :, :].rearrange("p s n t c -> p (s n t c)").bitcast(F32)
            quarter = 3 * GT * 512 // 4

            def h_zero(u):
                if isinstance(u.index, int) and u.index < 4:
                    pool.memset(wide_flat[:, u.index * quarter:(u.index + 1) * quarter], 0.0).then_inc(h_zeroed, 1)

            over_units(pool, UNITS, [(1, a_rstds), (2, a_final), (0, h_zero)])
            for i in range(2):
                pool.wait_ge(a_stored[i], 3 * SLOT_FULL)

            def rest(u, key, src, dst, r):
                pool.wait_ge(h_part[key][0], nth(u, 1, 1))
                if key == "q":
                    pool.wait_ge(h_part["v"][3], nth(u, 1, 1))
                elif u.has(1):
                    pool.wait_ge(h_part["q" if key == "v" else "k"][3], nth(u, 1, 0))
                pool.tensor_tensor(r, src, dst, ALU.subtract).then_inc(h_part[key][1], 1)

            def h_rests(u):
                rest(u, "k", by_e(h_k[:, u.slot]), in_e(h_kp[:, 0]), in_e(h_r[:, 0]))
                rest(u, "v", h_v[:, u.slot], h_vp[:, u.slot, 0], h_r[:, 1])
                pool.wait_ge(h_part["v"][2], nth(u, 1, 1))
                pool.tensor_tensor(h_vp[:, u.slot, 2], h_r[:, 1], h_vp[:, u.slot, 1], ALU.subtract).then_inc(h_part["v"][3], 1)

            def h_qrest(u):
                rest(u, "q", by_e(h_q[:, u.slot]), in_e(h_qp[:, 0]), in_e(h_r[:, 1]))

            over_units(pool, UNITS, [(2, h_qrest), (1, h_rests)])
            for i in range(2):
                pool.wait_ge(stored[i], 1 * SLOT_FULL)

            def m_rheads(u):
                if u.has(2):
                    pool.wait_ge(m_n1d, nth(u, 1, -1))
                rstd(u, m_msd, (m_ssd, nth(u, 1, 1)), m_ss[:, :], 1.0 / HD, RMS_EPS, m_ms[:, u.slot], m_rh[:, u.slot], TT * H, m_rhd)

            def m_rthird(u):
                if u.has(1):
                    pool.wait_ge(m_t3d, nth(u, 2, 0))
                rstd(u, m_m3d, (m_s3d, nth(u, 2, 2)), m_s3[:, :], 1.0 / D, RMS_EPS, m_m3[:, :], m_r3[:, :], TT, m_r3d)

            over_units(pool, UNITS, [(1, m_rheads), (2, m_rthird)])
            for i in range(2):
                pool.wait_ge(stored[i], 2 * SLOT_FULL)

            def c_rstds(u):
                if u.has(2):
                    pool.wait_ge(ln_norm, nth(u, 1, -1, 1))
                rstd(u, ln_ved, (ln_var, nth(u, 1, 1, 1)), c_mv[:, u.slot, :, 1], 1.0, LN_EPS,
                     c_ve[:, u.slot], c_rs[:, u.slot], TT, ln_rstd, 1)

            def c_natural(u):
                pool.wait_ge(c_cin[u.slot], landed(u))
                if u.has(2):
                    pool.wait_ge(c_o, nth(u, 1, -1))
                hi, lo = (flat(c_ch[u.slot][p][:, :, :]) for p in range(2))
                apart(pool)
                pool.tensor_scalar(hi, flat(c_c[:, u.slot]), 1.0, 0.0, ALU.mult, ALU.add).then_inc(c_cnhi, 1)
                pool.wait_ge(c_cnhi, nth(u, 1, 1))
                pool.tensor_tensor(lo, flat(c_c[:, u.slot]), hi.bitcast(F32), ALU.subtract).then_inc(c_cnlo, 1)

            def c_products(u):
                pool.wait_ge(ln_norm, nth(u, 1, 1, 1))
                if u.has(1):
                    pool.wait_ge(c_rd, nth(u, 1, 0))
                for i in range(TT):
                    ins = pool.tensor_tensor(c_rr[:, i], c_xn[:, u.slot, i], wbkrow[:, :], ALU.mult)
                ins.then_inc(c_rrd, 1)
                if u.has(2):
                    pool.wait_ge(c_yd, nth(u, 2, -2))
                pool.wait_ge(ln_in[u.slot], landed(u, 1, 1))
                for i in range(TT):
                    ins = pool.tensor_tensor(c_xb[:, u.slot, i], c_x[:, u.slot, i], bvrow[:, :], ALU.add)
                ins.then_inc(c_xbd, 1)

            over_units(pool, UNITS, [(1, c_rstds), (1, c_natural), (1, c_products)])
            for i in range(2):
                pool.wait_ge(stored[i], 3 * SLOT_FULL)

            def f_rstds(u):
                if u.has(2):
                    pool.wait_ge(ln_norm, nth(u, 1, -1, 2))
                rstd(u, ln_ved, (ln_var, nth(u, 1, 1, 2)), f_mv[:, u.slot, :, 1], 1.0, LN_EPS,
                     f_ve[:, u.slot], f_rs[:, u.slot], TT, ln_rstd, 2)

            def f_sums(j):
                def emit(u):
                    pool.wait_ge(f_h1d, nth(u, 4, j + 1))
                    pool.wait_ge(f_h2d, nth(u, 4, j + 1))
                    if j >= 2 or u.has(1):
                        pool.wait_ge(f_hlo, nth(u, 4, j - 1))
                    pool.tensor_tensor(f_hs[:, j % 2], f_h1[:, j % 2], f_h2[:, j % 2], ALU.add).then_inc(f_hsd, 1)
                return emit

            def f_bias(u):
                pool.wait_ge(f_top2, nth(u, 1, 1))
                apart(pool)
                for i in range(TT):
                    ins = pool.tensor_scalar(f_bo[:, i], borow[:, :], f_vs2[:, i:i + 1], 0.0, ALU.mult, ALU.add)
                ins.then_inc(f_bod, 1)
                pool.wait_ge(f_bod, nth(u, 1, 1))
                pool.wait_ge(ln_in[u.slot], landed(u, 1, 2))
                if u.has(2):
                    pool.wait_ge(f_yd, nth(u, 2, -2))
                pool.tensor_tensor(flat(f_xb[:, u.slot]), flat(f_bo[:, :, :]), flat(f_x[:, u.slot]), ALU.add).then_inc(f_xbd, 1)

            pool.wait_ge(s_w["small"], 16 * (N_SMALL + 1))
            over_units(pool, UNITS, [(1, f_rstds), (3, f_sums(0)), (3, f_sums(1)), (3, f_sums(2)), (3, f_sums(3)),
                                     (2, f_bias)])


_INS = ["x", "ctx_512", "L0_attn_Wq", "L0_attn_Wk", "L0_attn_Wv", "L0_attn_lambda_params", "L0_attn_g1",
        "L0_attn_g2", "L0_attn_g3", "L0_attn_W1", "L0_attn_W2", "L0_xattn_Wq", "L0_xattn_bq", "L0_xattn_Wk",
        "L0_xattn_bk", "L0_xattn_Wv", "L0_xattn_bv", "L0_ffn_wi", "L0_ffn_bi", "L0_ffn_wo", "L0_ffn_bo",
        "L0_ffn_lora_A", "L0_ffn_lora_B", "L0_ffn_gate_w", "L0_ffn_gate_b"]


def kernel(**inputs):
    import numpy as _np
    import concourse.bacc as _bacc
    from concourse import mybir as _mybir
    from concourse.bass_utils import run_bass_kernel_spmd as _run

    nc = _bacc.Bacc("TRN2", target_bir_lowering=False, num_devices=1)
    arrays, args = {}, []
    for name in _INS:
        a = _np.ascontiguousarray(inputs[name])
        arrays[f"in_{name}_dram"] = a
        args.append(nc.dram_tensor(f"in_{name}_dram", a.shape, _mybir.dt.from_np(a.dtype), kind="ExternalInput").ap())
    out = nc.dram_tensor("out_0_dram", (16, 256, 256), _mybir.dt.float32, kind="ExternalOutput").ap()
    decoder(nc, *args, out)
    r = _run(nc, [arrays], core_ids=[0])
    return r.results[0]["out_0_dram"]
```

```python
from contextlib import ExitStack

import numpy as np

import concourse.bass as bass
from concourse import mybir

F32 = mybir.dt.float32
F32R = mybir.dt.float32r
BF16 = mybir.dt.bfloat16
ALU = mybir.AluOpType
ACT = mybir.ActivationFunctionType
AX_X = mybir.AxisListType.X

P = 128
UNITS = 16
T = 256
TT = T // P
D = 256
KD = D // P
H, HD = 16, 16
GT = P // H
GROUPS = T // GT
C = 128
FF = 1024
FT = FF // P
EX, R = 8, 16
LN_EPS = 1e-5
RMS_EPS = float(np.finfo(np.float32).eps)
LAMBDA_INIT = 0.8 - 0.6 * float(np.exp(-0.3 * (1 - 1)))
HEAD_SCALE = 1.0 / float(np.sqrt(D // 2))


SLOT_FULL = 16 * (UNITS // 2)


class Unit:

    def __init__(self, pair, offset, least):
        self.pair, self.offset = pair, offset
        self.index = 2 * pair + offset
        self.slot = offset % 2
        self.turn = pair + offset // 2
        self.least = least

    def has(self, back):
        return self.least >= back

    def before(self, back):
        return Unit(self.pair, self.offset - back, self.least - back)


def nth(u, per_unit, k, loops=0):
    return u.index * per_unit + (k + loops * UNITS * per_unit)


def landed(u, dmas=1, loops=0):
    return u.turn * (16 * dmas) + 16 * dmas + loops * SLOT_FULL * dmas


def over_units(eng, units, stages):
    last = max(lag for lag, _ in stages)
    deepest = 4 if last <= 2 else 6
    assert last + 2 <= deepest and units % 2 == 0

    def step(t, pair=None):
        for lag, emit in stages:
            if pair is not None:
                emit(Unit(pair, t - lag, deepest - lag))
            elif 0 <= t - lag < units:
                emit(Unit(0, t - lag, t - lag))

    for t in range(deepest):
        step(t)
    with eng.Fori(deepest // 2, units // 2) as pair:
        for t in range(2):
            step(t, pair)
    for t in range(units, units + last):
        step(t)


def decoder(nc, x, ctx_512, Wq, Wk, Wv, lam, g1, g2, g3, W1, W2,
            xWq, xbq, xWk, xbk, xWv, xbv, wi, bi, wo, bo, lora_A, lora_B, gate_w, gate_b, out):
    assert x.shape == (UNITS, T, D)
    with ExitStack() as ctx:
        names = set()

        def sb(name, shape, dt=F32, where=ctx):
            return where.enter_context(nc.sbuf_tensor(name, shape, dt))

        def sem(name):
            assert name not in names
            names.add(name)
            return ctx.enter_context(nc.semaphore(name))

        bank = [ctx.enter_context(nc.psum_tensor(f"bank{i}", [P, 512], F32)) for i in range(8)]

        def pair(name, shape, where=ctx):
            return [sb(name + "_hi", shape, F32R, where), sb(name + "_lo", shape, F32R, where)]

        wqkvT = pair("wqkvT", [P, KD, 3 * D])
        w1T = pair("w1T", [P, KD, D])
        w2T = pair("w2T", [P, KD, D])
        mT = pair("mT", [P, KD, C])
        xwv = pair("xwv", [P, D])
        wiT = pair("wiT", [P, KD, FF])
        woT = pair("woT", [P, FT, D])
        laT = pair("laT", [P, KD, P])
        lbT = pair("lbT", [P, FF])
        gwT = pair("gwT", [P, KD, P])
        identf = sb("identf", [P, P])
        identb = sb("identb", [P, P], BF16)
        g1c = sb("g1c", [P, KD])
        g2row = sb("g2row", [P, H, HD])
        g3row = sb("g3row", [P, D])
        bvrow = sb("bvrow", [P, D])
        gbrow = sb("gbrow", [P, EX])
        bic = sb("bic", [P, FT])
        wbkrow = sb("wbkrow", [P, D])
        bqbk = sb("bqbk", [P, 1])
        bqk = sb("bqk", [P, 1])
        qfac = sb("qfac", [P, 1])
        slotmask = sb("slotmask", [P, GT])
        tril = sb("tril", [P, EX, EX])
        mhalf = sb("mhalf", [P, GROUPS])

        qkv_d = nc.dram_tensor("qkv_scratch", (3, UNITS, T, D), F32).ap()
        w_d = nc.dram_tensor("attn_scratch", (UNITS, T, D), F32).ap()
        x1_d = nc.dram_tensor("x1_scratch", (UNITS, T, D), F32).ap()
        x2_d = nc.dram_tensor("x2_scratch", (UNITS, T, D), F32).ap()

        def tiles(dram):
            return dram.rearrange("u (i p) f -> u p i f", p=P)

        x_t, x1_t, x2_t, out_t, ctx_t = map(tiles, (x, x1_d, x2_d, out, ctx_512))

        MIX = 3 * 1024 + 26 * 256 + 2 * 3 * GT * 512 // 2
        PROJECT = MIX - 37 * 256
        CROSS = MIX - (48 * 256 + 112)

        def below(name, words, where):
            if words:
                sb("below_" + name, [P, words], F32, where)

        with ExitStack() as a:
            n_in = sb("n_in", [P, 2, D], F32, a)
            nat = {"q": n_in}
            for key in ("k", "v", "w1", "w2", "xq"):
                nat[key] = sb("n_" + key, [P, 2, D], F32, a)
            nat["xk"] = sb("n_xk", [P, 1, D], F32, a)
            nat["xv"] = sb("n_xv", [P, 1, D], F32, a)
            nat["wi"] = sb("n_wi", [P, FT, D], F32, a)
            nat["wo"] = sb("n_wo", [P, 2, FF], F32, a)
            nat["la"] = sb("n_la", [P, 1, D], F32, a)
            nat["gw"] = sb("n_gw", [P, 1, D], F32, a)
            nat["lb"] = sb("n_lb", [P, FT, EX, R], F32, a)
            lamt = sb("lamt", [P, 4], F32, a)
            lprod = sb("lprod", [P, 2], F32, a)
            lexp = sb("lexp", [P, 2], F32, a)
            ldiff = sb("ldiff", [P, 1], F32, a)
            g2raw = sb("g2raw", [P, H, HD], F32, a)
            bqc = sb("bqc", [P, 2], F32, a)
            bkc = sb("bkc", [P, 2], F32, a)
            bkwide = sb("bkwide", [P, 2, P], F32, a)
            onesw = sb("onesw", [P, P], F32, a)
            xqT = sb("xqT", [P, 2, D], F32, a)
            xkT = sb("xkT", [P, 2, C], F32, a)
        s_w = {k: sem("w_" + k) for k in ("g1", "qkv", "early", "late", "lb", "small", "rows")}
        s_const, s_cleared = sem("const_made"), sem("const_cleared")
        s_gclear = sem("gate_cleared")
        s_turn = sem("weight_turned")
        s_whi = sem("weight_hi")
        s_wlo = sem("weight_lo")
        s_lam = sem("lambda_step")
        s_lamexp = sem("lambda_exp")
        s_small = sem("small_made")
        s_fold = sem("fold_turned")
        s_foldc = sem("fold_copied")
        s_foldm = sem("fold_product")
        s_folde = sem("fold_evacuated")
        s_foldlo = sem("fold_lo")

        ln_in = [sem(f"ln_in{i}") for i in range(2)]
        ln_stats, ln_var, ln_ved, ln_rstd = sem("ln_stats"), sem("ln_var"), sem("ln_var_eps"), sem("ln_rstd")
        ln_norm, ln_turned, ln_hi, ln_lo = sem("ln_norm"), sem("ln_turned"), sem("ln_hi"), sem("ln_lo")
        a_stored = [sem(f"a_stored{i}") for i in range(2)]
        stored = [sem(f"stored{i}") for i in range(2)]

        with ExitStack() as a:
            below("project", PROJECT, a)
            xin = sb("xin", [P, 2, TT, D], F32, a)
            a_st = sb("a_st", [P, 2, TT, 6], F32, a)
            a_mv = sb("a_mv", [P, 2, TT, 2], F32, a)
            a_ve = sb("a_ve", [P, 2, TT], F32, a)
            a_rs = sb("a_rs", [P, 2, TT], F32, a)
            a_xn = sb("a_xn", [P, 2, TT, D], F32, a)
            a_xT = [pair(f"a_xT{i}", [P, KD, T], a) for i in range(2)]
            a_exp = sb("a_exp", [P, 2, 512], F32, a)
            a_elu = sb("a_elu", [P, 2, 512], F32, a)
            a_out = sb("a_out", [P, 2, TT, 3 * D], F32, a)
        a_qk, a_v, a_negd, a_expd = sem("a_qk"), sem("a_v"), sem("a_negd"), sem("a_expd")
        a_elud, a_fin, a_vcopy = sem("a_elud"), sem("a_fin"), sem("a_vcopy")

        with ExitStack() as a:
            h_k = sb("h_k", [P, 2, 512], F32, a)
            h_v = sb("h_v", [P, 2, 512], F32, a)
            h_q = sb("h_q", [P, 2, 512], F32, a)
            h_kp = sb("h_kp", [P, 3, 512], BF16, a)
            h_qp = sb("h_qp", [P, 3, 512], BF16, a)
            h_vp = sb("h_vp", [P, 2, 3, 512], BF16, a)
            h_mp = sb("h_mp", [P, 2, 3, 512], BF16, a)
            h_r = sb("h_r", [P, 3, 512], F32, a)
            h_w = sb("h_w", [P, 512], F32, a)
            h_qd = sb("h_qd", [P, 2, 3, GT, 512], BF16, a)
            h_kd = sb("h_kd", [P, 2, 3, GT, 512], BF16, a)
        h_kin = [sem(f"h_kin{i}") for i in range(2)]
        h_vin = [sem(f"h_vin{i}") for i in range(2)]
        h_qin = [sem(f"h_qin{i}") for i in range(2)]
        h_part = {k: [sem(f"h_{k}_{s}") for s in ("p1", "rest", "p2", "p3")] for k in "kvqm"}
        h_zeroed = sem("h_zeroed")
        h_kdd = [sem(f"h_kdd{i}") for i in range(2)]
        h_qdd = sem("h_qdd")
        h_kv, h_out, h_wd = sem("h_kv"), sem("h_out"), sem("h_wd")

        with ExitStack() as a:
            below("mix", MIX, a)
            m_w = sb("m_w", [P, 2, TT, D], F32, a)
            m_x = sb("m_x", [P, 2, TT, D], F32, a)
            m_sq = sb("m_sq", [P, TT, D], F32, a)
            m_ss = sb("m_ss", [P, TT * H], F32, a)
            m_ms = sb("m_ms", [P, 2, TT * H], F32, a)
            m_rh = sb("m_rh", [P, 2, TT * H], F32, a)
            m_n1 = sb("m_n1", [P, TT, D], F32, a)
            m_at = sb("m_at", [P, TT, D], F32, a)
            m_s3 = sb("m_s3", [P, TT], F32, a)
            m_m3 = sb("m_m3", [P, TT], F32, a)
            m_r3 = sb("m_r3", [P, TT], F32, a)
            m_t3 = sb("m_t3", [P, TT, D], F32, a)
            m_a2 = sb("m_a2", [P, 2, TT, D], F32, a)
            m_xa = sb("m_xa", [P, 2, TT, D], F32, a)
            m_aT = [pair(f"m_aT{i}", [P, KD, T], a) for i in range(2)]
            m_g = sb("m_g", [P, 512], F32, a)
            m_hT = [pair(f"m_hT{i}", [P, KD, T], a) for i in range(2)]
            m_y = sb("m_y", [P, 2, TT, D], F32, a)
        m_win = [sem(f"m_win{i}") for i in range(2)]
        m_xin = [sem(f"m_xin{i}") for i in range(2)]
        m_sqd, m_ssd, m_msd, m_rhd = sem("m_sqd"), sem("m_ssd"), sem("m_msd"), sem("m_rhd")
        m_n1d, m_atd, m_s3d, m_m3d, m_r3d = sem("m_n1d"), sem("m_atd"), sem("m_s3d"), sem("m_m3d"), sem("m_r3d")
        m_t3d, m_a2d, m_xad = sem("m_t3d"), sem("m_a2d"), sem("m_xad")
        m_turned, m_hi, m_lo = sem("m_turned"), sem("m_hi"), sem("m_lo")
        m_h, m_gelu, m_ghi, m_glo = sem("m_h"), sem("m_gelu"), sem("m_ghi"), sem("m_glo")
        m_o, m_yd = sem("m_o"), sem("m_yd")

        with ExitStack() as a:
            below("cross", CROSS, a)
            c_x = sb("c_x", [P, 2, TT, D], F32, a)
            c_c = sb("c_c", [P, 2, TT, C], F32, a)
            c_st = sb("c_st", [P, 2, TT, 6], F32, a)
            c_mv = sb("c_mv", [P, 2, TT, 2], F32, a)
            c_ve = sb("c_ve", [P, 2, TT], F32, a)
            c_rs = sb("c_rs", [P, 2, TT], F32, a)
            c_xn = sb("c_xn", [P, 2, TT, D], F32, a)
            c_xb = sb("c_xb", [P, 2, TT, D], F32, a)
            c_rr = sb("c_rr", [P, TT, D], F32, a)
            c_r = sb("c_r", [P, 2, TT], F32, a)
            c_xT = [pair(f"c_xT{i}", [P, KD, T], a) for i in range(2)]
            c_ch = [pair(f"c_ch{i}", [P, TT, C], a) for i in range(2)]
            c_cT = [pair(f"c_cT{i}", [P, T], a) for i in range(2)]
            c_uT = [pair(f"c_uT{i}", [P, T], a) for i in range(2)]
            c_mx = sb("c_mx", [P, TT], F32, a)
            c_mr = sb("c_mr", [P, TT], F32, a)
            c_nb = sb("c_nb", [P, TT], F32, a)
            c_p = sb("c_p", [P, TT, T], F32, a)
            c_sum = sb("c_sum", [P, TT], F32, a)
            c_inv = sb("c_inv", [P, TT], F32, a)
            c_pT = pair("c_pT", [P, TT, T], a)
            c_oT = pair("c_oT", [P, T], a)
            c_y = sb("c_y", [P, 2, TT, D], F32, a)
        c_cin = [sem(f"c_cin{i}") for i in range(2)]
        c_xbd, c_rd = sem("c_xbd"), sem("c_rd")
        c_cturned, c_chi, c_clo = sem("c_cturned"), sem("c_chi"), sem("c_clo")
        c_cnhi, c_cnlo = sem("c_cnhi"), sem("c_cnlo")
        c_u, c_uhi, c_ulo = sem("c_u"), sem("c_uhi"), sem("c_ulo")
        c_s, c_mxd, c_mrd, c_nbd, c_pd, c_invd = sem("c_s"), sem("c_mxd"), sem("c_mrd"), sem("c_nbd"), sem("c_pd"), sem("c_invd")
        c_pturned, c_phi, c_plo = sem("c_pturned"), sem("c_phi"), sem("c_plo")
        c_o, c_ohi, c_olo = sem("c_o"), sem("c_ohi"), sem("c_olo")
        c_f, c_yd = sem("c_f"), sem("c_yd")

        with ExitStack() as a:
            borow = sb("borow", [P, D], F32, a)
            f_xn = sb("f_xn", [P, 2, TT, D], F32, a)
            f_xT = [pair(f"f_xT{i}", [P, KD, T], a) for i in range(2)]
            f_adT = [pair(f"f_adT{i}", [P, 2, T], a) for i in range(2)]
            f_h1 = sb("f_h1", [P, 2, 512], F32, a)
            f_h2 = sb("f_h2", [P, 2, 512], F32, a)
            f_hs = sb("f_hs", [P, 2, 512], F32, a)
            f_y = sb("f_y", [P, 2, TT, D], F32, a)
        with ExitStack() as a:
            below("feed", MIX, a)
            f_x = sb("f_x", [P, 2, TT, D], F32, a)
            f_st = sb("f_st", [P, 2, TT, 6], F32, a)
            f_mv = sb("f_mv", [P, 2, TT, 2], F32, a)
            f_ve = sb("f_ve", [P, 2, TT], F32, a)
            f_rs = sb("f_rs", [P, 2, TT], F32, a)
            f_lT = sb("f_lT", [P, T], F32, a)
            f_a = sb("f_a", [P, 2, T], F32, a)
            f_lg = sb("f_lg", [P, TT, EX], F32, a)
            f_mx = sb("f_mx", [P, TT], F32, a)
            f_sh = sb("f_sh", [P, TT, EX], F32, a)
            f_ex = sb("f_ex", [P, TT, EX], F32, a)
            f_sm = sb("f_sm", [P, TT], F32, a)
            f_iv = sb("f_iv", [P, TT], F32, a)
            f_sc = sb("f_sc", [P, TT, EX], F32, a)
            f_gt = sb("f_gt", [P, TT, EX, EX], F32, a)
            f_eq = sb("f_eq", [P, TT, EX, EX], F32, a)
            f_rk = sb("f_rk", [P, TT, EX], F32, a)
            f_top = sb("f_top", [P, TT, EX], F32, a)
            f_vs = sb("f_vs", [P, 2, TT], F32, a)
            f_vk = sb("f_vk", [P, 2, TT], F32, a)
            f_vs2 = sb("f_vs2", [P, TT], F32, a)
            f_xb = sb("f_xb", [P, 2, TT, D], F32, a)
            f_m = sb("f_m", [P, 2, TT, EX, R], BF16, a)
            f_ad = sb("f_ad", [P, 2, T], F32, a)
            f_hT = [pair(f"f_hT{i}", [P, FT, T], a) for i in range(2)]
        f_la, f_lTd, f_ad_, f_lturned = sem("f_la"), sem("f_lTd"), sem("f_acopied"), sem("f_lturned")
        f_top1, f_exd, f_vsd, f_md = sem("f_top1"), sem("f_exd"), sem("f_vsd"), sem("f_md")
        f_mT, f_adm, f_adhi, f_adlo = sem("f_mT"), sem("f_adm"), sem("f_adhi"), sem("f_adlo")
        f_xbd = sem("f_xbd")
        f_base, f_more = sem("f_base"), sem("f_more")
        f_h1d, f_h2d, f_hsd, f_hhi, f_hlo = sem("f_h1d"), sem("f_h2d"), sem("f_hsd"), sem("f_hhi"), sem("f_hlo")
        f_vkd, f_o, f_yd = sem("f_vkd"), sem("f_o"), sem("f_yd")

        def blocks(key, rows, k):
            return [nat[key][:, m, k * P:(k + 1) * P] for m in rows]

        jobs = []
        for k in range(KD):
            jobs.append((blocks("q", (0, 1), k) + blocks("k", (0, 1), k), wqkvT, (k, 0, 512), k))
        for k in range(KD):
            jobs.append((blocks("v", (0, 1), k), wqkvT, (k, 512, 768), k))
        for key, dst in (("w1", w1T), ("w2", w2T)):
            jobs.append((blocks(key, (0, 1), 0) + blocks(key, (0, 1), 1), dst, None, None))
        EARLY = len(jobs)
        QKV = 2 * KD
        for k in range(KD):
            for half in range(2):
                jobs.append((blocks("wi", range(4 * half, 4 * half + 4), k), wiT, (k, 512 * half, 512 * half + 512), None))
        for j in range(0, FT, 2):
            jobs.append((blocks("wo", (0, 1), j) + blocks("wo", (0, 1), j + 1), woT, ("rows", j), None))
        jobs.append((blocks("la", (0,), 0) + blocks("la", (0,), 1), laT, None, None))
        jobs.append((blocks("gw", (0,), 0) + blocks("gw", (0,), 1), gwT, None, None))
        for half in range(2):
            jobs.append(([nat["lb"][:, j].rearrange("p e r -> p (e r)") for j in range(4 * half, 4 * half + 4)],
                         lbT, ("flat", 512 * half), None))

        def target(part, at):
            if at is None:
                return part[:, :, :].rearrange("p a b -> p (a b)")
            if at[0] == "rows":
                return part[:, at[1]:at[1] + 2, :].rearrange("p a b -> p (a b)")
            if at[0] == "flat":
                return part[:, at[1]:at[1] + 512]
            return part[:, at[0], at[1]:at[2]]

        N_QKV, N_EARLY, N_SMALL, N_LATE, N_ROWS = 4, 5, 4, 4, 4

        f_chain = sem("f_chain")
        s_passed = sem("waits_passed")

        def apart(eng):
            eng.sem_inc(s_passed, 1)

        def flat(ap):
            return ap.rearrange("p a b -> p (a b)")

        def by_e(ap):
            return ap.rearrange("p (g e) -> p e g", e=HD)

        def in_e(ap):
            return ap.rearrange("p (e g) -> p e g", e=HD)

        block = ctx.enter_context(nc.Block())

        @block.sync
        def _(sp):
            def first_two(load):
                for n in range(2):
                    load(Unit(0, n, n))

            def but_first_two(load):
                return lambda u: None if isinstance(u.index, int) and u.index < 2 else load(u)

            def with_last(emit):
                return lambda u: emit() if isinstance(u.index, int) and u.index == UNITS - 1 else None

            def load_x(u):
                if u.has(2):
                    sp.wait_ge(ln_norm, nth(u, 1, -1, 0))
                    apart(sp)
                sp.dma_start(xin[:, u.slot], x_t[u.index]).then_inc(ln_in[u.slot], 16)

            loads = [(nat["q"][:, m, :], Wq.rearrange("(h e) f -> e h f", e=HD)[8 * m:8 * m + 8]) for m in range(2)]
            loads += [(nat[k], w.rearrange("(m p) f -> p m f", p=P)) for k, w in
                      (("k", Wk), ("v", Wv), ("w1", W1), ("w2", W2), ("xq", xWq), ("xk", xWk), ("xv", xWv))]
            sp.dma_start(g1c[:, :], g1.rearrange("(k p) -> p k", p=P), allow_slow_non_contiguous=True).then_inc(s_w["g1"], 16)
            for n, (dst, src) in enumerate(loads):
                sp.dma_start(dst if len(dst.shape) < 3 else dst[:, :, :], src).then_inc(s_w["qkv" if n < N_QKV else "early"], 16)
            sp.wait_ge(s_gclear, 1)
            late = [(nat["wi"][:, :, :], wi.rearrange("(m p) d -> p m d", p=P)),
                    (nat["wo"][:, :, :], wo.rearrange("(m p) f -> p m f", p=P)),
                    (nat["la"][:, 0, :], lora_A.rearrange("e r d -> (e r) d")),
                    (nat["gw"][0:EX, 0, :], gate_w)]
            for dst, src in late:
                sp.dma_start(dst, src).then_inc(s_w["late"], 16)
            first_two(load_x)
            small = [
                     (lamt[:, :], lam.rearrange("(a n) -> a n", a=1).broadcast_to([P, 4])),
                     (g2raw[:, 0, :], g2.rearrange("(a n) -> a n", a=1).broadcast_to([P, HD])),
                     (bqc[:, :], xbq.rearrange("(k p) -> p k", p=P)),
                     (bkc[:, :], xbk.rearrange("(k p) -> p k", p=P))]
            for dst, src in small:
                sp.dma_start(dst, src, allow_slow_non_contiguous=True).then_inc(s_w["small"], 16)
            for e in range(EX):
                sp.dma_start(nat["lb"][:, :, e, :], lora_B[e].rearrange("(m p) r -> p m r", p=P)).then_inc(s_w["lb"], 16)
            rows = [
                     (g3row[:, :], g3.rearrange("(a n) -> a n", a=1).broadcast_to([P, D])),
                     (bvrow[:, :], xbv.rearrange("(a n) -> a n", a=1).broadcast_to([P, D])),
                     (gbrow[:, :], gate_b.rearrange("(a n) -> a n", a=1).broadcast_to([P, EX])),
                     (bic[:, :], bi.rearrange("(k p) -> p k", p=P))]
            for dst, src in rows:
                sp.dma_start(dst, src, allow_slow_non_contiguous=True).then_inc(s_w["rows"], 16)
            assert (len(loads), len(small), len(late)) == (N_QKV + N_EARLY, N_SMALL, N_LATE)
            assert len(rows) == N_ROWS
            def store_qkv(u):
                sp.wait_ge(a_fin, nth(u, 2 * 3, 6))
                sp.wait_ge(a_vcopy, nth(u, 1, 1))
                for s in range(3):
                    sp.dma_start(tiles(qkv_d[s])[u.index],
                                 a_out[:, u.slot, :, s * D:(s + 1) * D]).then_inc(a_stored[u.slot], 16)

            def regroup(u, s):
                return qkv_d[s, u.index].rearrange("(g t) (h e) -> t h g e", t=GT, e=HD)

            def load_kv(u):
                if u.has(2):
                    sp.wait_ge(h_part["k"][3], nth(u, 1, -1))
                    sp.wait_ge(h_part["v"][3], nth(u, 1, -1))
                    apart(sp)
                sp.wait_ge(a_stored[u.slot], landed(u, 3))
                apart(sp)
                for dst, s, landing in ((h_k, 1, h_kin), (h_v, 2, h_vin)):
                    sp.dma_start(dst[:, u.slot].rearrange("p (g e) -> p g e", e=HD), regroup(u, s)).then_inc(landing[u.slot], 16)

            def load_q(u):
                if u.has(2):
                    sp.wait_ge(h_part["q"][3], nth(u, 1, -1))
                apart(sp)
                sp.dma_start(h_q[:, u.slot].rearrange("p (g e) -> p g e", e=HD), regroup(u, 0)).then_inc(h_qin[u.slot], 16)

            def store_w(u):
                sp.wait_ge(h_wd, nth(u, 1, 1))
                apart(sp)
                sp.dma_start(w_d[u.index].rearrange("(g t) (h e) -> t h g e", t=GT, e=HD),
                             h_w[:, :].rearrange("p (g e) -> p g e", e=HD)).then_inc(stored[u.slot], 16)

            def spread_k(u):
                sp.wait_ge(h_part["k"][3], nth(u, 1, 1))
                if u.has(2):
                    apart(sp)
                    sp.wait_ge(h_kv, nth(u, 1, -1))
                apart(sp)
                for t in range(GT):
                    rows = slice(t * H, (t + 1) * H)
                    sp.dma_start(h_kd[rows, u.slot, :, t, :], h_kp[rows]).then_inc(h_kdd[u.slot], 16)

            def start_heads():
                sp.wait_ge(s_foldlo, 3)
                sp.wait_ge(s_wlo, len(jobs))
                first_two(load_kv)
                first_two(load_q)

            over_units(sp, UNITS, [(0, but_first_two(load_x)), (1, with_last(start_heads)), (2, store_qkv)])
            sp.wait_ge(h_zeroed, 1)
            def load_w(u):
                if u.has(2):
                    sp.wait_ge(m_n1d, nth(u, 1, -1))
                    apart(sp)
                sp.wait_ge(stored[u.slot], landed(u))
                apart(sp)
                sp.dma_start(m_w[:, u.slot], tiles(w_d)[u.index]).then_inc(m_win[u.slot], 16)

            def start_mix():
                sp.wait_ge(h_kv, UNITS)
                first_two(load_w)

            over_units(sp, UNITS, [(0, but_first_two(load_kv)), (0, but_first_two(load_q)), (1, spread_k),
                                   (3, with_last(start_mix)), (4, store_w)])

            def load_mx(u):
                if u.has(2):
                    sp.wait_ge(m_xad, nth(u, 1, -1))
                apart(sp)
                sp.dma_start(m_x[:, u.slot], x_t[u.index]).then_inc(m_xin[u.slot], 16)

            def store_x1(u):
                sp.wait_ge(m_yd, nth(u, 1, 1))
                apart(sp)
                sp.dma_start(x1_t[u.index], m_y[:, u.slot]).then_inc(stored[u.slot], 16)

            def load_x1(u):
                if u.has(2):
                    sp.wait_ge(c_xbd, nth(u, 1, -1))
                    apart(sp)
                    sp.wait_ge(ln_norm, nth(u, 1, -1, 1))
                    apart(sp)
                sp.wait_ge(stored[u.slot], landed(u, 1, 1))
                apart(sp)
                sp.dma_start(c_x[:, u.slot], x1_t[u.index]).then_inc(ln_in[u.slot], 16)

            def start_cross():
                first_two(load_x1)

            over_units(sp, UNITS, [(0, but_first_two(load_w)), (2, load_mx), (2, with_last(start_cross)), (4, store_x1)])

            def load_context(u):
                if u.has(2):
                    sp.wait_ge(c_cnlo, nth(u, 1, -1))
                    apart(sp)
                    sp.wait_ge(c_cturned, nth(u, 1, -1))
                apart(sp)
                sp.dma_start(c_c[:, u.slot], ctx_t[u.index]).then_inc(c_cin[u.slot], 16)

            def store_x2(u):
                sp.wait_ge(c_yd, nth(u, 2, 2))
                apart(sp)
                sp.dma_start(x2_t[u.index], c_y[:, u.slot]).then_inc(stored[u.slot], 16)

            def load_x2(u):
                if u.has(2):
                    sp.wait_ge(ln_norm, nth(u, 1, -1, 2))
                    apart(sp)
                    sp.wait_ge(f_xbd, nth(u, 1, -1))
                    apart(sp)
                sp.wait_ge(stored[u.slot], landed(u, 1, 2))
                apart(sp)
                sp.dma_start(f_x[:, u.slot], x2_t[u.index]).then_inc(ln_in[u.slot], 16)

            def start_feed():
                sp.wait_ge(ln_norm, 2 * UNITS)
                sp.dma_start(borow[:, :], bo.rearrange("(a n) -> a n", a=1).broadcast_to([P, D])).then_inc(s_w["rows"], 16)
                first_two(load_x2)

            over_units(sp, UNITS, [(1, load_context), (0, but_first_two(load_x1)), (2, with_last(start_feed)),
                                   (3, store_x2)])

            def store_out(u):
                sp.wait_ge(f_yd, nth(u, 2, 2))
                apart(sp)
                sp.dma_start(out_t[u.index], f_y[:, u.slot]).then_inc(stored[u.slot], 16)

            over_units(sp, UNITS, [(0, but_first_two(load_x2)), (4, store_out)])
            for i in range(2):
                sp.wait_ge(stored[i], 4 * SLOT_FULL)

        def product(pe, acc, left, right, first=True, last=True, skip=False):
            for n, (a, b) in enumerate(((1, 0), (0, 1), (0, 0))):
                ins = pe.matmul(acc, left(a), right(b), start=first and n == 0, stop=last and n == 2,
                                skip_group_check=skip)
            return ins

        @block.tensor
        def _(pe):
            pe.wait_ge(s_const, 1)
            pe.wait_ge(s_w["qkv"], 16 * N_QKV)

            def turn_weights(first, last):
                for n in range(first, last):
                    if n == QKV:
                        pe.wait_ge(s_w["early"], 16 * N_EARLY)
                    if n >= 4:
                        pe.wait_ge(s_wlo, n - 3)
                    for i, b in enumerate(jobs[n][0]):
                        ins = pe.transpose(bank[(n + 2) % 4][:, i * P:(i + 1) * P], b, identf[:, :])
                    ins.then_inc(s_turn, 1)

            turn_weights(0, EARLY)
            for k in range(2):
                for m in range(2):
                    pe.transpose(bank[4][:, k * D + m * P:k * D + (m + 1) * P],
                                 nat["xq"][:, m, k * P:(k + 1) * P], identf[:, :])
            for k in range(2):
                ins = pe.transpose(bank[5][:, k * C:(k + 1) * C], nat["xk"][:, 0, k * P:(k + 1) * P], identf[:, :])
            ins.then_inc(s_fold, 1)
            pe.wait_ge(s_w["late"], 16 * N_LATE)
            turn_weights(EARLY, len(jobs) - 2)
            pe.wait_ge(s_foldc, 2)
            pe.wait_ge(s_small, 2)
            for m in range(KD):
                for k in range(2):
                    pe.matmul(bank[6][:, m * C:(m + 1) * C], xqT[:, k, m * P:(m + 1) * P], xkT[:, k, :],
                              start=k == 0, stop=k == 1)
            for k in range(2):
                pe.matmul(bank[7][:, 0:D], bkwide[:, k, :], xqT[:, k, :], start=k == 0, stop=k == 1)
            for k in range(2):
                pe.matmul(bank[7][:, D:D + 1], bkwide[:, k, :], bqc[:, k:k + 1], start=k == 0, stop=k == 1)
            for k in range(2):
                ins = pe.matmul(bank[7][:, D + 8:D + 9], xkT[:, k, :], bqc[:, k:k + 1], start=k == 0, stop=k == 1)
            ins.then_inc(s_foldm, 1)
            pe.wait_ge(s_w["lb"], 16 * EX)
            turn_weights(len(jobs) - 2, len(jobs))
            pe.wait_ge(s_wlo, len(jobs) - 2)

            def turn(dst, tile):
                for k in range(KD):
                    for i in range(TT):
                        ins = pe.transpose(dst[:, k * T + i * P:k * T + (i + 1) * P],
                                           tile[:, i, k * P:(k + 1) * P], identf[:, :])
                return ins

            def turn_x(u):
                pe.wait_ge(ln_norm, nth(u, 1, 1, 0))
                if u.has(2):
                    pe.wait_ge(ln_lo, nth(u, 1, -1, 0))
                turn(bank[4 * u.slot], a_xn[:, u.slot]).then_inc(ln_turned, 1)

            def project(u):
                pe.wait_ge(ln_lo, nth(u, 1, 1, 0))
                pe.wait_ge(s_wlo, len(jobs))
                pe.wait_ge(s_foldlo, 3)
                if u.has(2):
                    pe.wait_ge(a_elud, nth(u, 2, -2))
                xT = a_xT[u.slot]
                for i in range(TT):
                    for k in range(KD):
                        ins = product(pe, bank[4 * u.slot + 1 + i][:, :],
                                      lambda p: xT[p][:, k, i * P:(i + 1) * P],
                                      lambda p: wqkvT[p][:, k, 0:512], k == 0, k == KD - 1)
                    ins.then_inc(a_qk, 1)

            def project_v(u):
                xT = a_xT[u.slot]
                if u.has(2):
                    pe.wait_ge(a_vcopy, nth(u, 1, -1))
                for i in range(TT):
                    for k in range(KD):
                        ins = product(pe, bank[4 * u.slot + 3][:, i * D:(i + 1) * D],
                                      lambda p: xT[p][:, k, i * P:(i + 1) * P],
                                      lambda p: wqkvT[p][:, k, 512:768], k == 0, k == KD - 1)
                ins.then_inc(a_v, 1)

            over_units(pe, UNITS, [(2, project), (1, turn_x), (2, project_v)])
            pe.wait_ge(a_elud, 2 * UNITS)
            pe.wait_ge(a_vcopy, UNITS)

            PAIRS = [(2, 0), (0, 2), (1, 1), (1, 0), (0, 1), (0, 0)]

            def grouped(acc, wide, parts):
                for g in range(GROUPS):
                    for n, (a, b) in enumerate(PAIRS):
                        ins = pe.matmul(acc[:, g * HD:(g + 1) * HD],
                                        wide[:, a].rearrange("p t c -> p (t c)")[:, g:GT * 512:GROUPS],
                                        parts[:, b, g * HD:(g + 1) * HD],
                                        start=n == 0, stop=n == len(PAIRS) - 1)
                return ins

            def heads_kv(u):
                pe.wait_ge(h_kdd[u.slot], landed(u, GT))
                pe.wait_ge(h_part["v"][3], nth(u, 1, 1))
                if u.has(2):
                    pe.wait_ge(h_part["m"][1], nth(u, 1, -1))
                grouped(bank[u.slot], h_kd[:, u.slot], h_vp[:, u.slot]).then_inc(h_kv, 1)

            def heads_out(u):
                pe.wait_ge(h_qdd, nth(u, 3, 3))
                pe.wait_ge(h_part["m"][3], nth(u, 1, 1))
                if u.has(2):
                    pe.wait_ge(h_wd, nth(u, 1, -1))
                grouped(bank[2 + u.slot], h_qd[:, u.slot], h_mp[:, u.slot]).then_inc(h_out, 1)

            over_units(pe, UNITS, [(2, heads_kv), (3, heads_out)])
            pe.wait_ge(h_wd, UNITS)

            def turn_attn(u):
                pe.wait_ge(m_a2d, nth(u, 1, 1))
                if u.has(2):
                    pe.wait_ge(m_lo, nth(u, 1, -1))
                turn(bank[u.slot], m_a2[:, u.slot]).then_inc(m_turned, 1)

            def hidden(u):
                pe.wait_ge(m_lo, nth(u, 1, 1))
                if u.has(2):
                    pe.wait_ge(m_gelu, nth(u, 1, -1))
                for f in range(KD):
                    for k in range(KD):
                        ins = product(pe, bank[2 + u.slot][:, f * T:(f + 1) * T],
                                      lambda p: w1T[p][:, k, f * P:(f + 1) * P],
                                      lambda p: m_aT[u.slot][p][:, k, :], k == 0, k == KD - 1)
                ins.then_inc(m_h, 1)

            def mixed(u):
                pe.wait_ge(m_glo, nth(u, 1, 1))
                if u.has(2):
                    pe.wait_ge(m_yd, nth(u, 1, -1))
                for i in range(TT):
                    for k in range(KD):
                        ins = product(pe, bank[4 + u.slot][:, i * D:(i + 1) * D],
                                      lambda p: m_hT[u.slot][p][:, k, i * P:(i + 1) * P],
                                      lambda p: w2T[p][:, k, :], k == 0, k == KD - 1)
                ins.then_inc(m_o, 1)

            over_units(pe, UNITS, [(4, hidden), (3, turn_attn), (4, mixed)])
            pe.wait_ge(m_yd, UNITS)

            def turn_context(u):
                pe.wait_ge(c_cin[u.slot], landed(u))
                if u.has(1):
                    pe.wait_ge(c_clo, nth(u, 1, 0))
                for i in range(TT):
                    ins = pe.transpose(bank[1][:, i * P:(i + 1) * P], c_c[:, u.slot, i, :], identf[:, :])
                ins.then_inc(c_cturned, 1)

            def turn_cx(u):
                pe.wait_ge(ln_norm, nth(u, 1, 1, 1))
                if u.has(1):
                    pe.wait_ge(ln_lo, nth(u, 1, 0, 1))
                turn(bank[0], c_xn[:, u.slot]).then_inc(ln_turned, 1)

            def queries(u):
                pe.wait_ge(ln_lo, nth(u, 1, 1, 1))
                if u.has(1):
                    pe.wait_ge(c_ulo, nth(u, 1, 0))
                for k in range(KD):
                    ins = product(pe, bank[2][:, 0:T], lambda p: mT[p][:, k, :],
                                  lambda p: c_xT[u.slot][p][:, k, :], k == 0, k == KD - 1)
                ins.then_inc(c_u, 1)

            def scores(u):
                pe.wait_ge(c_ulo, nth(u, 1, 1))
                pe.wait_ge(c_clo, nth(u, 1, 1))
                if u.has(1):
                    pe.wait_ge(c_pd, nth(u, 2, 0))
                for i in range(TT):
                    ins = product(pe, bank[3][:, i * T:(i + 1) * T],
                                  lambda p: c_uT[u.slot][p][:, i * P:(i + 1) * P],
                                  lambda p: c_cT[u.slot][p][:, :])
                ins.then_inc(c_s, 1)

            def turn_p(u):
                pe.wait_ge(c_pd, nth(u, 2, 2))
                if u.has(1):
                    pe.wait_ge(c_plo, nth(u, 1, 0))
                turn(bank[4], c_p).then_inc(c_pturned, 1)

            def value(u):
                pe.wait_ge(c_plo, nth(u, 1, 1))
                pe.wait_ge(c_cnlo, nth(u, 1, 1))
                if u.has(1):
                    pe.wait_ge(c_olo, nth(u, 1, 0))
                for k in range(TT):
                    ins = product(pe, bank[5][:, 0:T], lambda p: c_ch[u.slot][p][:, k, :],
                                  lambda p: c_pT[p][:, k, :], k == 0, k == TT - 1)
                ins.then_inc(c_o, 1)

            def crossed(u):
                pe.wait_ge(c_olo, nth(u, 1, 1))
                if u.has(2):
                    pe.wait_ge(c_yd, nth(u, 2, -2))
                for i in range(TT):
                    ins = product(pe, bank[6 + u.slot][:, i * D:(i + 1) * D],
                                  lambda p: c_oT[p][:, i * P:(i + 1) * P], lambda p: xwv[p][:, :])
                ins.then_inc(c_f, 1)

            over_units(pe, UNITS, [(2, turn_context), (2, queries), (3, turn_p), (2, scores), (3, value),
                                   (1, turn_cx), (3, crossed)])
            pe.wait_ge(c_yd, 2 * UNITS)

            def turn_f(u):
                pe.wait_ge(ln_norm, nth(u, 1, 1, 2))
                if u.has(1):
                    pe.wait_ge(ln_lo, nth(u, 1, 0, 2))
                turn(bank[0], f_xn[:, u.slot]).then_inc(ln_turned, 1)

            def adapters_in(u):
                pe.wait_ge(ln_lo, nth(u, 1, 1, 2))
                if u.has(1):
                    pe.wait_ge(f_ad_, nth(u, 1, 0))
                    pe.wait_ge(f_top1, nth(u, 1, 0))
                for n, w in enumerate((gwT, laT)):
                    for k in range(KD):
                        ins = product(pe, bank[1][:, n * T:(n + 1) * T], lambda p: w[p][:, k, :],
                                      lambda p: f_xT[u.slot][p][:, k, :], k == 0, k == KD - 1)
                ins.then_inc(f_la, 1)

            def turn_logits(u):
                pe.wait_ge(f_lTd, nth(u, 1, 1))
                pe.wait_ge(f_ad_, nth(u, 1, 1))
                for i in range(TT):
                    ins = pe.transpose(bank[1][:, i * P:(i + 1) * P], f_lT[:, i * P:(i + 1) * P], identf[:, :])
                ins.then_inc(f_lturned, 1)

            def turn_masks(u):
                pe.wait_ge(f_md, nth(u, 2, 2))
                if u.has(1):
                    pe.wait_ge(f_adm, nth(u, 3, 0))
                for m in range(2):
                    for i in range(TT):
                        ins = pe.matmul(bank[2][:, m * T + i * P:m * T + (i + 1) * P],
                                        f_m[:, m, i].rearrange("p e r -> p (e r)"), identb[:, :],
                                        start=True, stop=True)
                ins.then_inc(f_mT, 1)

            def hidden_first(u, j):
                if j == 0:
                    pe.wait_ge(f_adlo, nth(u, 1, 1))
                if u.has(1):
                    pe.wait_ge(f_h2d, nth(u, 4, j - 3))
                for c in range(2):
                    f = 2 * j + c
                    acc = bank[4 + j][:, c * T:(c + 1) * T]
                    for k in range(KD):
                        product(pe, acc, lambda p: wiT[p][:, k, f * P:(f + 1) * P],
                                lambda p: f_xT[u.slot][p][:, k, :], c == 0 and k == 0, False, True)
                    ins = product(pe, acc, lambda p: lbT[p][:, f * P:(f + 1) * P],
                                  lambda p: f_adT[u.slot][p][:, 0, :], False, False, True)
                ins.then_inc(f_base, 1)

            def hidden_second(u, j):
                pe.wait_ge(f_h1d, nth(u, 4, j + 1))
                for c in range(2):
                    f = 2 * j + c
                    ins = product(pe, bank[4 + j][:, c * T:(c + 1) * T],
                                  lambda p: lbT[p][:, f * P:(f + 1) * P],
                                  lambda p: f_adT[u.slot][p][:, 1, :], False, True, True)
                ins.then_inc(f_more, 1)

            def hidden_a(u):
                hidden_first(u, 0)
                hidden_first(u, 1)
                hidden_second(u, 0)

            def hidden_b(u):
                hidden_first(u, 2)
                hidden_second(u, 1)
                hidden_first(u, 3)
                hidden_second(u, 2)
                hidden_second(u, 3)

            def fed(j):
                def emit(u):
                    pe.wait_ge(f_hlo, nth(u, 4, j + 1))
                    if j == 0 and u.has(1):
                        pe.wait_ge(f_yd, nth(u, 2, 0))
                    for i in range(TT):
                        for f in (2 * j, 2 * j + 1):
                            ins = product(pe, bank[3][:, i * D:(i + 1) * D],
                                          lambda p: f_hT[u.slot][p][:, f, i * P:(i + 1) * P],
                                          lambda p: woT[p][:, f, :], i == 0 and f == 0, f == FT - 1, True)
                    if j == 3:
                        ins.then_inc(f_o, 1)
                return emit

            over_units(pe, UNITS, [(3, turn_masks), (2, turn_f), (4, fed(0)), (4, fed(1)), (4, fed(2)), (2, adapters_in),
                                   (4, fed(3)), (2, turn_logits), (3, hidden_a), (3, hidden_b)])

        @block.scalar
        def _(act):
            act.wait_ge(s_w["g1"], 16)

            def high_parts(first, last):
                for n in range(first, last):
                    blks, dst, at, k = jobs[n]
                    act.wait_ge(s_turn, n + 1)
                    act.activation(target(dst[0], at), bank[(n + 2) % 4][:, 0:len(blks) * P], ACT.Copy,
                                   scale=g1c[:, k:k + 1] if k is not None else 1.0).then_inc(s_whi, 1)

            high_parts(0, EARLY)
            act.wait_ge(s_fold, 1)
            act.activation(flat(xqT[:, :, :]), bank[4][:, :], ACT.Copy).then_inc(s_foldc, 1)
            act.activation(flat(xkT[:, :, :]), bank[5][:, 0:2 * C], ACT.Copy).then_inc(s_foldc, 1)
            high_parts(EARLY, len(jobs) - 2)
            act.wait_ge(s_lam, 1)
            act.activation(lexp[:, :], lprod[:, :], ACT.Exp).then_inc(s_lamexp, 1)
            act.wait_ge(s_foldm, 1)
            act.activation(flat(mT[0][:, :, :]), bank[6][:, 0:2 * C], ACT.Copy).then_inc(s_folde, 1)
            act.activation(wbkrow[:, :], bank[7][:, 0:D], ACT.Copy).then_inc(s_folde, 1)
            act.activation(bqbk[:, :], bank[7][:, D:D + 1], ACT.Copy).then_inc(s_folde, 1)
            act.activation(bqk[:, :], bank[7][:, D + 8:D + 9], ACT.Copy).then_inc(s_folde, 1)
            act.activation(xwv[0][:, :], nat["xv"][:, 0, :], ACT.Copy).then_inc(s_folde, 1)
            high_parts(len(jobs) - 2, len(jobs))

            def a_split(u):
                act.wait_ge(ln_turned, nth(u, 1, 1, 0))
                if u.has(2):
                    act.wait_ge(a_v, nth(u, 1, -1))
                act.activation(flat(a_xT[u.slot][0][:, :, :]), bank[4 * u.slot][:, :], ACT.Copy).then_inc(ln_hi, 1)

            def a_exps(i):
                def emit(u):
                    b = bank[4 * u.slot + 1 + i]
                    act.wait_ge(a_qk, nth(u, 2, i + 1))
                    if u.has(1):
                        act.wait_ge(a_elud, nth(u, 2, i - 1))
                    act.activation(a_exp[:, i], b[:, :], ACT.Relu, scale=-1.0).then_inc(a_negd, 1)
                    act.wait_ge(a_negd, nth(u, 2, i + 1))
                    act.activation(a_exp[:, i], a_exp[:, i], ACT.Exp, scale=-1.0).then_inc(a_expd, 1)
                return emit

            def a_values(u):
                act.wait_ge(a_v, nth(u, 1, 1))
                if u.has(2):
                    act.wait_ge(a_stored[u.slot], u.turn * 48)
                act.activation(a_out[:, u.slot, :, 2 * D:3 * D],
                               bank[4 * u.slot + 3][:, :].rearrange("p (i d) -> p i d", i=TT),
                               ACT.Copy).then_inc(a_vcopy, 1)

            over_units(act, UNITS, [(2, a_exps(0)), (2, a_exps(1)), (1, a_split), (2, a_values)])

            def part1(key, dst, src):
                act.activation(dst, src, ACT.Copy).then_inc(h_part[key][0], 1)

            def part2(u, key, dst, r):
                act.wait_ge(h_part[key][1], nth(u, 1, 1))
                act.activation(dst[:, 1], h_r[:, r], ACT.Copy).then_inc(h_part[key][2], 1)

            def kv_parts(u):
                act.wait_ge(h_kin[u.slot], landed(u))
                if u.has(1):
                    act.wait_ge(h_kdd[u.before(1).slot], landed(u.before(1), GT))
                part1("k", in_e(h_kp[:, 0]), by_e(h_k[:, u.slot]))

            def kv_rest(u):
                act.wait_ge(h_vin[u.slot], landed(u))
                if u.has(2):
                    act.wait_ge(h_kv, nth(u, 1, -1))
                part1("v", h_vp[:, u.slot, 0], h_v[:, u.slot])
                part2(u, "k", h_kp, 0)
                part2(u, "v", h_vp[:, u.slot], 1)

            def q_parts(u):
                act.wait_ge(h_qin[u.slot], landed(u))
                if u.has(1):
                    act.wait_ge(h_qdd, nth(u, 3, 0))
                part1("q", in_e(h_qp[:, 0]), by_e(h_q[:, u.slot]))

            def q_second(u):
                part2(u, "q", h_qp, 1)

            def m_parts(u):
                act.wait_ge(h_kv, nth(u, 1, 1))
                if u.has(2):
                    act.wait_ge(h_out, nth(u, 1, -1))
                part1("m", h_mp[:, u.slot, 0], bank[u.slot][:, :])
                part2(u, "m", h_mp[:, u.slot], 2)

            def w_copy(u):
                act.wait_ge(h_out, nth(u, 1, 1))
                if u.has(1):
                    act.wait_ge(stored[u.before(1).slot], landed(u.before(1)))
                act.activation(h_w[:, :], bank[2 + u.slot][:, :], ACT.Copy).then_inc(h_wd, 1)

            over_units(act, UNITS, [(2, q_parts), (1, kv_parts), (2, q_second), (1, kv_rest), (4, w_copy), (2, m_parts)])

            def m_squares(u):
                act.wait_ge(m_win[u.slot], landed(u))
                if u.has(1):
                    act.wait_ge(m_ssd, nth(u, 1, 0))
                act.activation(flat(m_sq[:, :, :]), flat(m_w[:, u.slot]), ACT.Square).then_inc(m_sqd, 1)

            def m_squares3(u):
                act.wait_ge(m_atd, nth(u, 1, 1))
                if u.has(1):
                    act.wait_ge(m_m3d, nth(u, 1, 0))
                    act.wait_ge(m_t3d, nth(u, 2, 0))
                for i in range(TT):
                    act.activation(m_t3[:, i], m_at[:, i], ACT.Square, accum_out=m_s3[:, i:i + 1]).then_inc(m_s3d, 1)

            def m_split(u):
                act.wait_ge(m_turned, nth(u, 1, 1))
                if u.has(2):
                    act.wait_ge(m_h, nth(u, 1, -1))
                act.activation(flat(m_aT[u.slot][0][:, :, :]), bank[u.slot][:, :], ACT.Copy).then_inc(m_hi, 1)

            def m_gelus(u):
                act.wait_ge(m_h, nth(u, 1, 1))
                if u.has(1):
                    act.wait_ge(m_glo, nth(u, 1, 0))
                act.activation(m_g[:, :], bank[2 + u.slot][:, :], ACT.Gelu).then_inc(m_gelu, 1)
                act.wait_ge(m_gelu, nth(u, 1, 1))
                if u.has(2):
                    act.wait_ge(m_o, nth(u, 1, -1))
                act.activation(flat(m_hT[u.slot][0][:, :, :]), m_g[:, :], ACT.Copy).then_inc(m_ghi, 1)

            over_units(act, UNITS, [(4, m_gelus), (3, m_split), (2, m_squares3), (0, m_squares)])

            def c_context(u):
                act.wait_ge(c_cturned, nth(u, 1, 1))
                if u.has(2):
                    act.wait_ge(c_s, nth(u, 1, -1))
                act.activation(c_cT[u.slot][0][:, :], bank[1][:, 0:T], ACT.Copy).then_inc(c_chi, 1)

            def c_queries(u):
                act.wait_ge(c_u, nth(u, 1, 1))
                if u.has(2):
                    act.wait_ge(c_s, nth(u, 1, -1))
                act.activation(c_uT[u.slot][0][:, :], bank[2][:, 0:T], ACT.Identity, bias=bqk[:, 0:1]).then_inc(c_uhi, 1)

            def c_split(u):
                act.wait_ge(ln_turned, nth(u, 1, 1, 1))
                if u.has(2):
                    act.wait_ge(c_u, nth(u, 1, -1))
                act.activation(flat(c_xT[u.slot][0][:, :, :]), bank[0][:, :], ACT.Copy).then_inc(ln_hi, 1)

            def c_exps(u):
                act.wait_ge(c_nbd, nth(u, 1, 1))
                if u.has(1):
                    act.wait_ge(c_pturned, nth(u, 1, 0))
                    act.wait_ge(c_invd, nth(u, 1, 0))
                for i in range(TT):
                    act.activation(c_p[:, i], bank[3][:, i * T:(i + 1) * T], ACT.Exp, bias=c_nb[:, i:i + 1],
                                   accum_out=c_sum[:, i:i + 1]).then_inc(c_pd, 1)

            def c_psplit(u):
                act.wait_ge(c_pturned, nth(u, 1, 1))
                if u.has(1):
                    act.wait_ge(c_o, nth(u, 1, 0))
                act.activation(flat(c_pT[0][:, :, :]), bank[4][:, :], ACT.Copy).then_inc(c_phi, 1)

            def c_osplit(u):
                act.wait_ge(c_o, nth(u, 1, 1))
                if u.has(1):
                    act.wait_ge(c_f, nth(u, 1, 0))
                act.activation(c_oT[0][:, :], bank[5][:, 0:T], ACT.Copy).then_inc(c_ohi, 1)

            over_units(act, UNITS, [(2, c_context), (2, c_queries), (3, c_psplit), (3, c_osplit), (1, c_split), (2, c_exps)])

            def f_split(u):
                act.wait_ge(ln_turned, nth(u, 1, 1, 2))
                if u.has(2):
                    act.wait_ge(f_base, nth(u, 4, -4))
                act.activation(flat(f_xT[u.slot][0][:, :, :]), bank[0][:, :], ACT.Copy).then_inc(ln_hi, 1)

            def f_adapters(u):
                act.wait_ge(f_la, nth(u, 1, 1))
                if u.has(1):
                    act.wait_ge(f_lturned, nth(u, 1, 0))
                act.activation(f_lT[:, :], bank[1][:, 0:T], ACT.Copy).then_inc(f_lTd, 1)
                if u.has(2):
                    act.wait_ge(f_adm, nth(u, 3, -3))
                act.activation(f_a[:, u.slot], bank[1][:, T:2 * T], ACT.Copy).then_inc(f_ad_, 1)

            def f_exps(u):
                act.wait_ge(f_top1, nth(u, 1, 1))
                if u.has(1):
                    act.wait_ge(f_xbd, nth(u, 1, 0))
                act.activation(flat(f_ex[:, :, :]), flat(f_sh[:, :, :]), ACT.Exp).then_inc(f_exd, 1)

            def relus(u, j, ready, out_slot, done, back):
                act.wait_ge(ready, nth(u, 4, j + 1))
                if j >= 2 or u.has(1):
                    act.wait_ge(f_hsd, nth(u, 4, j - 1))
                for c in range(2):
                    f = 2 * j + c
                    ins = act.activation(out_slot[:, j % 2, c * T:(c + 1) * T], bank[4 + j][:, c * T:(c + 1) * T],
                                         ACT.Relu, bias=bic[:, f:f + 1])
                ins.then_inc(done, 1)

            def relus_a(u):
                relus(u, 0, f_base, f_h1, f_h1d, 0)
                relus(u, 1, f_base, f_h1, f_h1d, 0)
                relus(u, 0, f_more, f_h2, f_h2d, 0)

            def relus_b(u):
                relus(u, 1, f_more, f_h2, f_h2d, 0)
                relus(u, 2, f_base, f_h1, f_h1d, 0)
                relus(u, 3, f_base, f_h1, f_h1d, 0)
                relus(u, 2, f_more, f_h2, f_h2d, 0)
                relus(u, 3, f_more, f_h2, f_h2d, 0)

            act.wait_ge(s_w["rows"], 16 * N_ROWS)
            over_units(act, UNITS, [(2, f_split), (2, f_adapters), (2, f_exps), (3, relus_a), (3, relus_b)])

        @block.vector
        def _(dve):
            dve.memset(mhalf[:, :], -0.5)
            dve.memset(nat["gw"][:, 0, :], 0.0).then_inc(s_gclear, 1)
            dve.memset(onesw[:, :], 1.0).then_inc(s_small, 1)

            def low_parts(first, last):
                for n in range(first, last):
                    blks, dst, at, k = jobs[n]
                    dve.wait_ge(s_whi, n + 1)
                    turned, hi = bank[(n + 2) % 4][:, 0:len(blks) * P], target(dst[0], at).bitcast(F32)
                    if k is None:
                        dve.tensor_tensor(target(dst[1], at), turned, hi, ALU.subtract).then_inc(s_wlo, 1)
                    else:
                        dve.scalar_tensor_tensor(out=target(dst[1], at), in0=turned, scalar=g1c[:, k:k + 1], in1=hi,
                                                 op0=ALU.mult, op1=ALU.subtract).then_inc(s_wlo, 1)

            low_parts(0, len(jobs) - 2)
            dve.wait_ge(s_w["small"], 16 * N_SMALL)
            dve.tensor_tensor(lprod[:, :], lamt[:, 0:4:2], lamt[:, 1:4:2], ALU.mult).then_inc(s_lam, 1)
            dve.wait_ge(s_small, 1)
            for k in range(2):
                ins = dve.tensor_scalar(bkwide[:, k, :], onesw[:, :], bkc[:, k:k + 1], None, ALU.mult)
            ins.then_inc(s_small, 1)
            dve.tensor_scalar(g2row[:, :, :], g2raw[:, 0:1, :].broadcast_to([P, H, HD]), 1.0 - LAMBDA_INIT, None, ALU.mult)
            def moments(u, loops, src, st, mv):
                dve.wait_ge(ln_in[u.slot], landed(u, 1, loops))
                for i in range(TT):
                    ins = dve.bn_stats(st[:, u.slot, i, :], src[:, u.slot, i, :])
                ins.then_inc(ln_stats, 1)
                dve.wait_ge(ln_stats, nth(u, 1, 1, loops))
                apart(dve)
                for i in range(TT):
                    ins = dve.bn_aggr(mv[:, u.slot, i, :], st[:, u.slot, i, :])
                ins.then_inc(ln_var, 1)

            def normalise(u, loops, src, mv, rs, dst):
                dve.wait_ge(ln_rstd, nth(u, 1, 1, loops))
                for i in range(TT):
                    ins = dve.tensor_scalar(dst[:, u.slot, i, :], src[:, u.slot, i, :], mv[:, u.slot, i, 0:1],
                                            rs[:, u.slot, i:i + 1], ALU.subtract, ALU.mult)
                ins.then_inc(ln_norm, 1)

            def low(u, hi_done, hi, lo, src, done, loops=0):
                dve.wait_ge(hi_done, nth(u, 1, 1, loops))
                dve.tensor_tensor(lo, src, hi.bitcast(F32), ALU.subtract).then_inc(done, 1)

            def a_moments(u):
                moments(u, 0, xin, a_st, a_mv)

            def a_normalise(u):
                if u.has(2):
                    dve.wait_ge(ln_turned, nth(u, 1, -1, 0))
                normalise(u, 0, xin, a_mv, a_rs, a_xn)

            def a_low(u):
                low(u, ln_hi, flat(a_xT[u.slot][0][:, :, :]), flat(a_xT[u.slot][1][:, :, :]),
                    bank[4 * u.slot][:, :], ln_lo)

            def a_elus(i):
                def emit(u):
                    dve.wait_ge(a_expd, nth(u, 2, i + 1))
                    if u.has(1):
                        dve.wait_ge(a_fin, nth(u, 6, 3 * i - 3))
                    dve.scalar_tensor_tensor(out=a_elu[:, i], in0=bank[4 * u.slot + 1 + i][:, :], scalar=0.0,
                                             in1=a_exp[:, i], op0=ALU.max, op1=ALU.add).then_inc(a_elud, 1)
                return emit

            def prepare_rest(u):
                if not isinstance(u.index, int) or u.index:
                    return
                dve.wait_ge(s_lamexp, 1)
                dve.tensor_tensor(ldiff[:, :], lexp[:, 1:2], lexp[:, 0:1], ALU.subtract).then_inc(s_lam, 1)
                dve.wait_ge(s_lam, 2)
                dve.tensor_scalar(qfac[:, :], ldiff[:, :], LAMBDA_INIT, HEAD_SCALE, ALU.subtract, ALU.mult).then_inc(s_foldlo, 1)
                dve.wait_ge(s_folde, 5)
                dve.tensor_tensor(flat(mT[1][:, :, :]), bank[6][:, 0:2 * C], flat(mT[0][:, :, :]).bitcast(F32),
                                  ALU.subtract).then_inc(s_foldlo, 1)
                dve.tensor_tensor(xwv[1][:, :], nat["xv"][:, 0, :], xwv[0][:, :].bitcast(F32), ALU.subtract).then_inc(s_foldlo, 1)
                low_parts(len(jobs) - 2, len(jobs))

            over_units(dve, UNITS, [(1, a_moments), (1, a_normalise), (1, prepare_rest), (2, a_elus(0)), (1, a_low), (2, a_elus(1))])

            def rest(u, key, src, dst, r):
                dve.wait_ge(h_part[key][0], nth(u, 1, 1))
                if u.has(1):
                    dve.wait_ge(h_part[key][3], nth(u, 1, 0))
                dve.tensor_tensor(h_r[:, r], src, dst[:, 0], ALU.subtract).then_inc(h_part[key][1], 1)

            def part3(u, key, dst, r):
                dve.wait_ge(h_part[key][2], nth(u, 1, 1))
                dve.tensor_tensor(dst[:, 2], h_r[:, r], dst[:, 1], ALU.subtract).then_inc(h_part[key][3], 1)

            def k_part3(u):
                part3(u, "k", h_kp, 0)

            def q_part3(u):
                part3(u, "q", h_qp, 1)

            def m_rest(u):
                dve.wait_ge(h_kv, nth(u, 1, 1))
                rest(u, "m", bank[u.slot][:, :], h_mp[:, u.slot], 2)

            def m_part3(u):
                part3(u, "m", h_mp[:, u.slot], 2)

            def spread_q(part):
                def emit(u):
                    dve.wait_ge(h_part["q"][(0, 2, 3)[part]], nth(u, 1, 1))
                    if part == 0 and u.has(2):
                        dve.wait_ge(h_out, nth(u, 1, -1))
                    if part == 0 and isinstance(u.index, int) and u.index == 0:
                        for i in range(2):
                            dve.wait_ge(a_stored[i], 3 * SLOT_FULL)
                    for t in range(GT):
                        ins = dve.tensor_scalar(h_qd[:, u.slot, part, t, :], h_qp[:, part], slotmask[:, t:t + 1],
                                                None, ALU.mult)
                    ins.then_inc(h_qdd, 1)
                return emit

            over_units(dve, UNITS, [(2, spread_q(0)), (2, q_part3), (1, k_part3), (2, spread_q(1)), (2, spread_q(2)),
                                    (2, m_rest), (2, m_part3)])

            def m_sums(u):
                dve.wait_ge(m_sqd, nth(u, 1, 1))
                if u.has(1):
                    dve.wait_ge(m_msd, nth(u, 1, 0))
                dve.tensor_reduce(m_ss[:, :], m_sq[:, :, :].rearrange("p i (h e) -> p (i h) e", e=HD),
                                  AX_X, ALU.add).then_inc(m_ssd, 1)

            def m_heads(u):
                dve.wait_ge(m_rhd, nth(u, 1, 1))
                wide = m_rh[:, u.slot].rearrange("p (n o) -> p n o", o=1).broadcast_to([P, TT * H, HD])
                dve.tensor_tensor(m_n1[:, :, :].rearrange("p i (h e) -> p (i h) e", e=HD),
                                  m_w[:, u.slot].rearrange("p i (h e) -> p (i h) e", e=HD), wide, ALU.mult).then_inc(m_n1d, 1)
                dve.wait_ge(m_n1d, nth(u, 1, 1))
                if u.has(1):
                    dve.wait_ge(m_a2d, nth(u, 1, 0))
                for i in range(TT):
                    ins = dve.tensor_tensor(m_at[:, i], m_n1[:, i], g2row[:, :, :].rearrange("p h e -> p (h e)"), ALU.mult)
                ins.then_inc(m_atd, 1)

            def m_third(u):
                dve.wait_ge(m_r3d, nth(u, 1, 1))
                dve.wait_ge(m_s3d, nth(u, 2, 2))
                for i in range(TT):
                    ins = dve.scalar_tensor_tensor(out=m_t3[:, i], in0=m_at[:, i], scalar=m_r3[:, i:i + 1],
                                                   in1=g3row[:, :], op0=ALU.mult, op1=ALU.mult)
                    ins.then_inc(m_t3d, 1)

            def m_sum(u):
                dve.wait_ge(m_t3d, nth(u, 2, 2))
                if u.has(2):
                    dve.wait_ge(m_turned, nth(u, 1, -1))
                dve.tensor_tensor(flat(m_a2[:, u.slot]), flat(m_t3[:, :, :]), flat(m_at[:, :, :]), ALU.add).then_inc(m_a2d, 1)

            def m_with_x(u):
                dve.wait_ge(m_xin[u.slot], landed(u))
                dve.wait_ge(m_a2d, nth(u, 1, 1))
                if u.has(2):
                    dve.wait_ge(m_yd, nth(u, 1, -1))
                dve.tensor_tensor(flat(m_xa[:, u.slot]), flat(m_a2[:, u.slot]), flat(m_x[:, u.slot]), ALU.add).then_inc(m_xad, 1)

            def m_low(u):
                low(u, m_hi, flat(m_aT[u.slot][0][:, :, :]), flat(m_aT[u.slot][1][:, :, :]), bank[u.slot][:, :], m_lo)

            def m_gsplit(u):
                hi, lo = (flat(m_hT[u.slot][p][:, :, :]) for p in range(2))
                dve.wait_ge(m_ghi, nth(u, 1, 1))
                dve.tensor_tensor(lo, m_g[:, :], hi.bitcast(F32), ALU.subtract).then_inc(m_glo, 1)

            def m_residual(u):
                dve.wait_ge(m_o, nth(u, 1, 1))
                dve.wait_ge(m_xad, nth(u, 1, 1))
                if u.has(2):
                    dve.wait_ge(stored[u.slot], u.turn * 16 + 1 * SLOT_FULL)
                dve.tensor_tensor(flat(m_y[:, u.slot]), bank[4 + u.slot][:, :], flat(m_xa[:, u.slot]), ALU.add).then_inc(m_yd, 1)

            dve.wait_ge(s_w["rows"], 16 * N_ROWS)
            over_units(dve, UNITS, [(3, m_third), (3, m_sum), (2, m_heads), (4, m_gsplit), (3, m_low), (3, m_with_x),
                                    (4, m_residual), (0, m_sums)])

            def c_moments(u):
                moments(u, 1, c_x, c_st, c_mv)

            def c_normalise(u):
                if u.has(2):
                    dve.wait_ge(ln_turned, nth(u, 1, -1, 1))
                normalise(u, 1, c_x, c_mv, c_rs, c_xn)

            def c_constant(u):
                for i in range(TT):
                    ins = dve.scalar_tensor_tensor(out=c_rr[:, i], in0=c_xn[:, u.slot, i], scalar=1.0, in1=wbkrow[:, :],
                                                   op0=ALU.mult, op1=ALU.mult, accum_out=c_r[:, u.slot, i:i + 1])
                ins.then_inc(c_rd, 1)

            def c_clow(u):
                low(u, c_chi, c_cT[u.slot][0][:, :], c_cT[u.slot][1][:, :], bank[1][:, 0:T], c_clo)

            def c_low(u):
                low(u, ln_hi, flat(c_xT[u.slot][0][:, :, :]), flat(c_xT[u.slot][1][:, :, :]), bank[0][:, :], ln_lo, 1)

            def c_usplit(u):
                dve.wait_ge(c_uhi, nth(u, 1, 1))
                dve.scalar_tensor_tensor(out=c_uT[u.slot][1][:, :], in0=bank[2][:, 0:T], scalar=bqk[:, 0:1],
                                         in1=c_uT[u.slot][0][:, :].bitcast(F32), op0=ALU.add,
                                         op1=ALU.subtract).then_inc(c_ulo, 1)

            def c_max(u):
                dve.wait_ge(c_s, nth(u, 1, 1))
                dve.tensor_reduce(c_mx[:, :], bank[3][:, :].rearrange("p (i k) -> p i k", i=TT),
                                  AX_X, ALU.max).then_inc(c_mxd, 1)
                dve.wait_ge(c_mxd, nth(u, 1, 1))
                dve.wait_ge(c_rd, nth(u, 1, 1))
                dve.scalar_tensor_tensor(out=c_mr[:, :], in0=c_r[:, u.slot], scalar=bqbk[:, 0:1], in1=c_mx[:, :],
                                         op0=ALU.add, op1=ALU.add).then_inc(c_mrd, 1)
                dve.wait_ge(c_mrd, nth(u, 1, 1))
                if u.has(1):
                    dve.wait_ge(c_pd, nth(u, 2, 0))
                dve.scalar_tensor_tensor(out=c_nb[:, :], in0=c_r[:, u.slot], scalar=bqbk[:, 0:1], in1=c_mr[:, :],
                                         op0=ALU.add, op1=ALU.subtract).then_inc(c_nbd, 1)

            def c_plow(u):
                dve.wait_ge(c_pd, nth(u, 2, 2))
                if u.has(1):
                    dve.wait_ge(c_yd, nth(u, 2, 0))
                dve.reciprocal(c_inv[:, :], c_sum[:, :]).then_inc(c_invd, 1)
                low(u, c_phi, flat(c_pT[0][:, :, :]), flat(c_pT[1][:, :, :]), bank[4][:, :], c_plo)

            def c_olow(u):
                low(u, c_ohi, c_oT[0][:, :], c_oT[1][:, :], bank[5][:, 0:T], c_olo)

            def c_residual(u):
                dve.wait_ge(c_f, nth(u, 1, 1))
                dve.wait_ge(c_xbd, nth(u, 1, 1))
                dve.wait_ge(c_invd, nth(u, 1, 1))
                if u.has(2):
                    dve.wait_ge(stored[u.slot], u.turn * 16 + 2 * SLOT_FULL)
                for i in range(TT):
                    dve.scalar_tensor_tensor(out=c_y[:, u.slot, i], in0=bank[6 + u.slot][:, i * D:(i + 1) * D],
                                             scalar=c_inv[:, i:i + 1], in1=c_xb[:, u.slot, i],
                                             op0=ALU.mult, op1=ALU.add).then_inc(c_yd, 1)

            over_units(dve, UNITS, [(1, c_moments), (2, c_clow), (2, c_usplit), (3, c_plow), (1, c_normalise),
                                    (2, c_constant), (2, c_max), (3, c_olow), (1, c_low), (3, c_residual)])

            def f_moments(u):
                moments(u, 2, f_x, f_st, f_mv)

            def f_normalise(u):
                if u.has(2):
                    dve.wait_ge(ln_turned, nth(u, 1, -1, 2))
                normalise(u, 2, f_x, f_mv, f_rs, f_xn)

            def f_low(u):
                low(u, ln_hi, flat(f_xT[u.slot][0][:, :, :]), flat(f_xT[u.slot][1][:, :, :]), bank[0][:, :], ln_lo, 2)

            chain = {"n": 0, "sem": f_chain}
            LINKS = 11

            def link(u, ins):
                chain["n"] += 1
                ins.then_inc(chain["sem"], 1)
                dve.wait_ge(chain["sem"], nth(u, LINKS, chain["n"]))

            def f_shift(u):
                chain["n"] = 0
                dve.wait_ge(f_lturned, nth(u, 1, 1))
                link(u, dve.tensor_tensor(f_lg[:, :, :], bank[1][:, 0:TT * P].rearrange("p (i e) -> p i e", i=TT)[:, :, 0:EX],
                                          gbrow[:, :].rearrange("p (o e) -> p o e", o=1).broadcast_to([P, TT, EX]), ALU.add))
                link(u, dve.tensor_reduce(f_mx[:, :], f_lg[:, :, :], AX_X, ALU.max))
                dve.tensor_tensor(f_sh[:, :, :], f_lg[:, :, :],
                                  f_mx[:, :].rearrange("p (i o) -> p i o", o=1).broadcast_to([P, TT, EX]),
                                  ALU.subtract).then_inc(f_top1, 1)

            def f_rank(u):
                dve.wait_ge(f_exd, nth(u, 1, 1))
                link(u, dve.tensor_reduce(f_sm[:, :], f_ex[:, :, :], AX_X, ALU.add))
                link(u, dve.reciprocal(f_iv[:, :], f_sm[:, :]))
                ins = dve.tensor_tensor(f_sc[:, :, :], f_ex[:, :, :],
                                        f_iv[:, :].rearrange("p (i o) -> p i o", o=1).broadcast_to([P, TT, EX]), ALU.mult)
                link(u, ins)
                for i in range(TT):
                    mine = f_sc[:, i, :].rearrange("p (e o) -> p e o", o=1).broadcast_to([P, EX, EX])
                    other = f_sc[:, i, :].rearrange("p (o j) -> p o j", o=1).broadcast_to([P, EX, EX])
                    dve.tensor_tensor(f_gt[:, i], other, mine, ALU.is_gt)
                    ins = dve.tensor_tensor(f_eq[:, i], other, mine, ALU.is_equal)
                link(u, ins)
                for i in range(TT):
                    ins = dve.tensor_tensor(f_eq[:, i], f_eq[:, i], tril[:, :, :], ALU.mult)
                link(u, ins)
                link(u, dve.tensor_tensor(f_gt[:, :, :, :].rearrange("p i e j -> p (i e j)"),
                                          f_gt[:, :, :, :].rearrange("p i e j -> p (i e j)"),
                                          f_eq[:, :, :, :].rearrange("p i e j -> p (i e j)"), ALU.add))
                link(u, dve.tensor_reduce(f_rk[:, :, :].rearrange("p i e -> p (i e)"),
                                          f_gt[:, :, :, :].rearrange("p i e j -> p (i e) j"), AX_X, ALU.add))
                if u.has(1):
                    dve.wait_ge(f_mT, nth(u, 1, 0))
                for m in range(2):
                    for i in range(TT):
                        ins = dve.tensor_scalar(f_m[:, m, i],
                                                f_rk[:, i, :].rearrange("p (e o) -> p e o", o=1).broadcast_to([P, EX, R]),
                                                float(m), None, ALU.is_equal)
                    ins.then_inc(f_md, 1)
                link(u, dve.scalar_tensor_tensor(out=flat(f_top[:, :, :]), in0=flat(f_rk[:, :, :]), scalar=1.5,
                                                 in1=flat(f_sc[:, :, :]), op0=ALU.is_lt, op1=ALU.mult))
                ins = dve.tensor_reduce(f_vs[:, u.slot], f_top[:, :, :], AX_X, ALU.add)
                ins.then_inc(f_vsd, 1)
                dve.wait_ge(f_vsd, nth(u, 1, 1))
                link(u, dve.tensor_scalar(f_vs2[:, :], f_vs[:, u.slot], 2.0, None, ALU.mult))
                assert chain["n"] == LINKS
                if u.has(2):
                    dve.wait_ge(f_yd, nth(u, 2, -2))
                for i in range(TT):
                    ins = dve.scalar_tensor_tensor(out=f_xb[:, u.slot, i], in0=borow[:, :], scalar=f_vs2[:, i:i + 1],
                                                   in1=f_x[:, u.slot, i], op0=ALU.mult, op1=ALU.add)
                ins.then_inc(f_xbd, 1)

            def f_masked(u):
                dve.wait_ge(f_mT, nth(u, 1, 1))
                dve.wait_ge(f_ad_, nth(u, 1, 1))
                if u.has(1):
                    dve.wait_ge(f_adlo, nth(u, 1, 0))
                for m in range(2):
                    dve.tensor_tensor(f_ad[:, m], f_a[:, u.slot], bank[2][:, m * T:(m + 1) * T], ALU.mult).then_inc(f_adm, 1)
                dve.wait_ge(f_adm, nth(u, 3, 2))
                dve.tensor_tensor(f_ad[:, 1], f_ad[:, 1], f_ad[:, 0], ALU.subtract).then_inc(f_adm, 1)
                dve.wait_ge(f_adm, nth(u, 3, 3))
                if u.has(2):
                    dve.wait_ge(f_more, nth(u, 4, -4))
                hi, lo = (flat(f_adT[u.slot][p][:, :, :]) for p in range(2))
                dve.tensor_copy(hi, flat(f_ad[:, :, :])).then_inc(f_adhi, 1)
                dve.wait_ge(f_adhi, nth(u, 1, 1))
                dve.tensor_tensor(lo, flat(f_ad[:, :, :]), hi.bitcast(F32), ALU.subtract).then_inc(f_adlo, 1)

            def hidden_split(j):
                def emit(u):
                    dve.wait_ge(f_hsd, nth(u, 4, j + 1))
                    if j == 0 and u.has(2):
                        dve.wait_ge(f_o, nth(u, 1, -1))
                    hi, lo = (flat(f_hT[u.slot][p][:, 2 * j:2 * j + 2, :]) for p in range(2))
                    dve.tensor_copy(hi, f_hs[:, j % 2]).then_inc(f_hhi, 1)
                    dve.wait_ge(f_hhi, nth(u, 4, j + 1))
                    dve.tensor_tensor(lo, f_hs[:, j % 2], hi.bitcast(F32), ALU.subtract).then_inc(f_hlo, 1)
                return emit

            def f_keep(u):
                if u.has(2):
                    dve.wait_ge(f_yd, nth(u, 2, -2))
                dve.tensor_copy(f_vk[:, u.slot], f_vs[:, u.slot]).then_inc(f_vkd, 1)

            def f_residual(i):
                def emit(u):
                    dve.wait_ge(f_vkd, nth(u, 1, 1))
                    dve.wait_ge(f_o, nth(u, 1, 1))
                    if i == 0:
                        dve.wait_ge(f_xbd, nth(u, 1, 1))
                        if u.has(2):
                            dve.wait_ge(stored[u.slot], u.turn * 16 + 3 * SLOT_FULL)
                    dve.scalar_tensor_tensor(out=f_y[:, u.slot, i], in0=bank[3][:, i * D:(i + 1) * D],
                                             scalar=f_vk[:, u.slot, i:i + 1], in1=f_xb[:, u.slot, i],
                                             op0=ALU.mult, op1=ALU.add).then_inc(f_yd, 1)
                return emit

            dve.wait_ge(s_w["rows"], 16 * (N_ROWS + 1))
            over_units(dve, UNITS, [(2, f_low), (4, hidden_split(3)), (3, f_masked), (3, f_keep), (1, f_moments), (4, f_residual(0)),
                                    (4, f_residual(1)), (2, f_shift), (1, f_normalise), (2, f_rank),
                                    (3, hidden_split(0)), (3, hidden_split(1)), (3, hidden_split(2))])

        @block.gpsimd
        def _(pool):
            pool.memset(identf[:, :], 0.0).then_inc(s_cleared, 1)
            pool.memset(tril[:, :, :], 1.0).then_inc(s_cleared, 1)
            pool.memset(slotmask[:, :], 1.0).then_inc(s_cleared, 1)
            pool.wait_ge(s_cleared, 3)
            pool.affine_select(out=identf[:, :], in_=identf[:, :], compare_op=ALU.not_equal, fill=1.0, base=0,
                               pattern=[[-1, P]], channel_multiplier=1).then_inc(s_const, 1)
            pool.affine_select(out=tril[:, :, :], in_=tril[:, :, :], compare_op=ALU.is_gt, fill=0.0, base=0,
                               pattern=[[1, EX], [-1, EX]], channel_multiplier=0)
            pool.affine_select(out=slotmask[:, :], in_=slotmask[:, :], compare_op=ALU.is_ge, fill=0.0, base=0,
                               pattern=[[-H, GT]], channel_multiplier=1).then_inc(s_cleared, 1)
            pool.wait_ge(s_cleared, 4)
            pool.affine_select(out=slotmask[:, :], in_=slotmask[:, :], compare_op=ALU.is_gt, fill=0.0, base=H,
                               pattern=[[H, GT]], channel_multiplier=-1)
            pool.wait_ge(s_const, 1)
            pool.tensor_copy(identb[:, :], identf[:, :])
            pool.memset(h_kd[:, :, :, :, :].rearrange("p s n t c -> p (s n t c)").bitcast(F32), 0.0).then_inc(h_zeroed, 1)

            def rstd(u, step_sem, ready, src, scale, add, tmp, out_ap, width, done, loops=0):
                pool.wait_ge(*ready)
                apart(pool)
                pool.tensor_scalar(tmp, src, scale, add, ALU.mult, ALU.add).then_inc(step_sem, 1)
                pool.wait_ge(step_sem, nth(u, 1, 1, loops))
                pool.tensor_tensor(out_ap, tmp, mhalf[:, 0:width], ALU.pow).then_inc(done, 1)


            def a_rstds(u):
                if u.has(2):
                    pool.wait_ge(ln_norm, nth(u, 1, -1, 0))
                rstd(u, ln_ved, (ln_var, nth(u, 1, 1, 0)), a_mv[:, u.slot, :, 1], 1.0 + RMS_EPS, RMS_EPS * LN_EPS,
                     a_ve[:, u.slot], a_rs[:, u.slot], TT, ln_rstd, 0)

            def a_final(u):
                for i in range(TT):
                    pool.wait_ge(a_elud, nth(u, 2, i + 1))
                    if i == 0 and not u.has(1):
                        pool.wait_ge(s_foldlo, 1)
                    if i == 0 and u.has(2):
                        pool.wait_ge(a_stored[u.slot], u.turn * 48)
                    apart(pool)
                    for lo, hi, fac in ((0, P, HEAD_SCALE), (P, D, qfac[:, 0:1]), (D, 2 * D, 1.0)):
                        pool.tensor_scalar(a_out[:, u.slot, i, lo:hi], a_elu[:, i, lo:hi], -1.0, fac,
                                           ALU.add, ALU.mult).then_inc(a_fin, 1)

            over_units(pool, UNITS, [(1, a_rstds), (2, a_final)])

            def rest(u, key, src, dst, r):
                pool.wait_ge(h_part[key][0], nth(u, 1, 1))
                if key == "q":
                    pool.wait_ge(h_part["v"][3], nth(u, 1, 1))
                elif u.has(1):
                    pool.wait_ge(h_part["q" if key == "v" else "k"][3], nth(u, 1, 0))
                pool.tensor_tensor(r, src, dst, ALU.subtract).then_inc(h_part[key][1], 1)

            def h_rests(u):
                rest(u, "k", by_e(h_k[:, u.slot]), in_e(h_kp[:, 0]), in_e(h_r[:, 0]))
                rest(u, "v", h_v[:, u.slot], h_vp[:, u.slot, 0], h_r[:, 1])
                pool.wait_ge(h_part["v"][2], nth(u, 1, 1))
                pool.tensor_tensor(h_vp[:, u.slot, 2], h_r[:, 1], h_vp[:, u.slot, 1], ALU.subtract).then_inc(h_part["v"][3], 1)

            def h_qrest(u):
                rest(u, "q", by_e(h_q[:, u.slot]), in_e(h_qp[:, 0]), in_e(h_r[:, 1]))

            over_units(pool, UNITS, [(2, h_qrest), (1, h_rests)])

            def m_rheads(u):
                if u.has(2):
                    pool.wait_ge(m_n1d, nth(u, 1, -1))
                rstd(u, m_msd, (m_ssd, nth(u, 1, 1)), m_ss[:, :], 1.0 / HD, RMS_EPS, m_ms[:, u.slot], m_rh[:, u.slot], TT * H, m_rhd)

            def m_rthird(u):
                if u.has(1):
                    pool.wait_ge(m_t3d, nth(u, 2, 0))
                rstd(u, m_m3d, (m_s3d, nth(u, 2, 2)), m_s3[:, :], 1.0 / D, RMS_EPS, m_m3[:, :], m_r3[:, :], TT, m_r3d)

            over_units(pool, UNITS, [(1, m_rheads), (2, m_rthird)])

            def c_rstds(u):
                if u.has(2):
                    pool.wait_ge(ln_norm, nth(u, 1, -1, 1))
                rstd(u, ln_ved, (ln_var, nth(u, 1, 1, 1)), c_mv[:, u.slot, :, 1], 1.0, LN_EPS,
                     c_ve[:, u.slot], c_rs[:, u.slot], TT, ln_rstd, 1)

            def c_natural(u):
                pool.wait_ge(c_cin[u.slot], landed(u))
                if u.has(2):
                    pool.wait_ge(c_o, nth(u, 1, -1))
                hi, lo = (flat(c_ch[u.slot][p][:, :, :]) for p in range(2))
                apart(pool)
                pool.tensor_scalar(hi, flat(c_c[:, u.slot]), 1.0, 0.0, ALU.mult, ALU.add).then_inc(c_cnhi, 1)
                pool.wait_ge(c_cnhi, nth(u, 1, 1))
                pool.tensor_tensor(lo, flat(c_c[:, u.slot]), hi.bitcast(F32), ALU.subtract).then_inc(c_cnlo, 1)

            def c_with_bias(u):
                if u.has(2):
                    pool.wait_ge(c_yd, nth(u, 2, -2))
                pool.wait_ge(ln_in[u.slot], landed(u, 1, 1))
                for i in range(TT):
                    ins = pool.tensor_tensor(c_xb[:, u.slot, i], c_x[:, u.slot, i], bvrow[:, :], ALU.add)
                ins.then_inc(c_xbd, 1)

            pool.wait_ge(s_w["rows"], 16 * N_ROWS)
            over_units(pool, UNITS, [(1, c_rstds), (2, c_with_bias), (2, c_natural)])

            def f_rstds(u):
                if u.has(2):
                    pool.wait_ge(ln_norm, nth(u, 1, -1, 2))
                rstd(u, ln_ved, (ln_var, nth(u, 1, 1, 2)), f_mv[:, u.slot, :, 1], 1.0, LN_EPS,
                     f_ve[:, u.slot], f_rs[:, u.slot], TT, ln_rstd, 2)

            def f_sums(j):
                def emit(u):
                    pool.wait_ge(f_h1d, nth(u, 4, j + 1))
                    pool.wait_ge(f_h2d, nth(u, 4, j + 1))
                    if j >= 2 or u.has(1):
                        pool.wait_ge(f_hlo, nth(u, 4, j - 1))
                    pool.tensor_tensor(f_hs[:, j % 2], f_h1[:, j % 2], f_h2[:, j % 2], ALU.add).then_inc(f_hsd, 1)
                return emit

            over_units(pool, UNITS, [(1, f_rstds), (3, f_sums(0)), (3, f_sums(1)), (3, f_sums(2)), (3, f_sums(3))])


_INS = ["x", "ctx_512", "L0_attn_Wq", "L0_attn_Wk", "L0_attn_Wv", "L0_attn_lambda_params", "L0_attn_g1",
        "L0_attn_g2", "L0_attn_g3", "L0_attn_W1", "L0_attn_W2", "L0_xattn_Wq", "L0_xattn_bq", "L0_xattn_Wk",
        "L0_xattn_bk", "L0_xattn_Wv", "L0_xattn_bv", "L0_ffn_wi", "L0_ffn_bi", "L0_ffn_wo", "L0_ffn_bo",
        "L0_ffn_lora_A", "L0_ffn_lora_B", "L0_ffn_gate_w", "L0_ffn_gate_b"]


def kernel(**inputs):
    import numpy as _np
    import concourse.bacc as _bacc
    from concourse import mybir as _mybir
    from concourse.bass_utils import run_bass_kernel_spmd as _run

    nc = _bacc.Bacc("TRN2", target_bir_lowering=False, num_devices=1)
    arrays, args = {}, []
    for name in _INS:
        a = _np.ascontiguousarray(inputs[name])
        arrays[f"in_{name}_dram"] = a
        args.append(nc.dram_tensor(f"in_{name}_dram", a.shape, _mybir.dt.from_np(a.dtype), kind="ExternalInput").ap())
    out = nc.dram_tensor("out_0_dram", (16, 256, 256), _mybir.dt.float32, kind="ExternalOutput").ap()
    decoder(nc, *args, out)
    r = _run(nc, [arrays], core_ids=[0])
    return r.results[0]["out_0_dram"]
```
